# Optimizing a Trainium2 kernel written in Bass

```python
import numpy as np
import jax
import jax.numpy as jnp

def _softmax(x, axis=-1):
    return jax.nn.softmax(x, axis=axis)

def _gelu(x):
    return jax.nn.gelu(x, approximate=True)

def _silu(x):
    return jax.nn.silu(x)

def _sigmoid(x):
    return jax.nn.sigmoid(x)

def _layernorm(x, axis=-1, eps=1e-05):
    m = jnp.mean(x, axis=axis, keepdims=True)
    v = jnp.var(x, axis=axis, keepdims=True)
    return (x - m) / jnp.sqrt(v + eps)

def _scatter_add(tgt, idx, src, axis=0):
    return tgt.at[idx].add(src)

def _segment_sum(src, seg, n):
    return jax.ops.segment_sum(src, seg, n)
kernel_name = 'mk_cond_seq_d2_seqx_r4_e687b3'

def setup_inputs(seed: int=0):
    np.random.seed(seed)
    _w = jnp.asarray

    def _rec_inputs():
        import jax
        import jax.numpy as jnp
        _rk = jax.random.key(seed)
        x = -0.0002928 + 1 * jax.random.normal(jax.random.fold_in(_rk, 1), (8, 512, 256), jnp.float32)
        _lenS = 512 - jax.random.randint(jax.random.fold_in(_rk, 7), (8,), 0, max(1, 512 // 4) + 1, jnp.int32)
        _lenS2 = 512 - jax.random.randint(jax.random.fold_in(_rk, 8), (8,), 0, max(1, 512 // 4) + 1, jnp.int32)
        cond_1024 = 0.0061147 + 1.02565 * jax.random.normal(jax.random.fold_in(_rk, 11), (8, 256), jnp.float32)
        return (x, cond_1024)
    x, cond_1024 = _rec_inputs()

    def _L0_cond_setup():
        import jax, jax.numpy as jnp
        import numpy as np
        D = 256
        H = 16
        HD = 4 * D
        B, T = (4, 256)
        EPS = 1e-05

        def _layernorm(x, g, b):
            mu = jnp.mean(x, axis=-1, keepdims=True)
            var = jnp.mean(jnp.square(x - mu), axis=-1, keepdims=True)
            return (x - mu) * jax.lax.rsqrt(var + EPS) * g + b

        def _attention(x, Wqkv, Wproj, bproj):
            b, t, c = x.shape
            hd = c // H
            qkv = (x @ Wqkv).reshape(b, t, 3, H, hd).transpose(2, 0, 3, 1, 4)
            q, k, v = (qkv[0], qkv[1], qkv[2])
            scale = hd ** (-0.5)
            scores = jnp.einsum('bhqd,bhkd->bhqk', q, k) * scale
            causal = jnp.tril(jnp.ones((t, t), bool))
            scores = jnp.where(causal, scores, -jnp.inf)
            attn = jax.nn.softmax(scores, axis=-1)
            out = jnp.einsum('bhqk,bhkd->bhqd', attn, v)
            out = out.transpose(0, 2, 1, 3).reshape(b, t, c)
            return out @ Wproj + bproj
        key = jax.random.key(seed)
        ks = jax.random.split(key, 12)
        s = 0.02
        return {'x': jax.random.normal(ks[0], (B, T, D), jnp.float32), 'condition': jax.random.normal(ks[1], (B, D), jnp.float32), 'Wqkv': jax.random.normal(ks[2], (D, 3 * D), jnp.float32) * s, 'Wproj': jax.random.normal(ks[3], (D, D), jnp.float32) * s, 'bproj': jnp.zeros((D,), jnp.float32), 'W1': jax.random.normal(ks[4], (D, HD), jnp.float32) * s, 'b1': jnp.zeros((HD,), jnp.float32), 'W2': jax.random.normal(ks[5], (HD, D), jnp.float32) * s, 'b2': jnp.zeros((D,), jnp.float32), 'g1': jnp.ones((D,), jnp.float32), 'be1': jnp.zeros((D,), jnp.float32), 'g2': jnp.ones((D,), jnp.float32), 'be2': jnp.zeros((D,), jnp.float32), 'Wada': jax.random.normal(ks[6], (D, 6 * D), jnp.float32) * s, 'bada': jax.random.normal(ks[7], (6 * D,), jnp.float32) * s}
    _L0_cond_all = _L0_cond_setup()
    _L0_cond_in = {k: v for k, v in _L0_cond_all.items() if k in ('Wqkv', 'Wproj', 'bproj', 'W1', 'b1', 'W2', 'b2', 'g1', 'be1', 'g2', 'be2', 'Wada', 'bada')}
    del _L0_cond_all

    def _L1_cond_setup():
        import jax, jax.numpy as jnp
        import numpy as np
        EPS = 1e-05

        def _sln(h, w, ln_g, ln_b, Wg, bg, Wb, bb):
            mu = jnp.mean(h, axis=-1, keepdims=True)
            var = jnp.mean((h - mu) ** 2, axis=-1, keepdims=True)
            ln = (h - mu) / jnp.sqrt(var + EPS) * ln_g + ln_b
            gamma = (w @ Wg.T + bg)[:, None, :]
            beta = (w @ Wb.T + bb)[:, None, :]
            return gamma * ln + beta
        key = jax.random.key(seed)
        ks = jax.random.split(key, 20)
        B, N, D = (4, 256, 256)
        F = 4 * D
        s = lambda fan: 1.0 / np.sqrt(fan)
        inp = {'hidden': jax.random.normal(ks[0], (B, N, D), jnp.float32), 'w': jax.random.normal(ks[1], (B, D), jnp.float32), 'ln_g': jnp.ones((D,), jnp.float32), 'ln_b': jnp.zeros((D,), jnp.float32), 'Wg': jax.random.normal(ks[2], (D, D), jnp.float32) * s(D), 'bg': jnp.zeros((D,), jnp.float32), 'Wb': jax.random.normal(ks[3], (D, D), jnp.float32) * s(D), 'bb': jnp.zeros((D,), jnp.float32), 'Wqkv': jax.random.normal(ks[4], (3 * D, D), jnp.float32) * s(D), 'bqkv': jnp.zeros((3 * D,), jnp.float32), 'Wp': jax.random.normal(ks[5], (D, D), jnp.float32) * s(D), 'bp': jnp.zeros((D,), jnp.float32), 'W1': jax.random.normal(ks[6], (F, D), jnp.float32) * s(D), 'b1': jnp.zeros((F,), jnp.float32), 'W2': jax.random.normal(ks[7], (D, F), jnp.float32) * s(F), 'b2': jnp.zeros((D,), jnp.float32), 'num_heads': 16}
        return inp
    _L1_cond_all = _L1_cond_setup()
    _L1_cond_in = {k: v for k, v in _L1_cond_all.items() if k in ('ln_g', 'ln_b', 'Wg', 'bg', 'Wb', 'bb', 'Wqkv', 'bqkv', 'Wp', 'bp', 'W1', 'b1', 'W2', 'b2')}
    del _L1_cond_all
    return {'x': x, 'cond_1024': cond_1024, 'L0_cond_Wqkv': _L0_cond_in['Wqkv'], 'L0_cond_Wproj': _L0_cond_in['Wproj'], 'L0_cond_bproj': _L0_cond_in['bproj'], 'L0_cond_W1': _L0_cond_in['W1'], 'L0_cond_b1': _L0_cond_in['b1'], 'L0_cond_W2': _L0_cond_in['W2'], 'L0_cond_b2': _L0_cond_in['b2'], 'L0_cond_g1': _L0_cond_in['g1'], 'L0_cond_be1': _L0_cond_in['be1'], 'L0_cond_g2': _L0_cond_in['g2'], 'L0_cond_be2': _L0_cond_in['be2'], 'L0_cond_Wada': _L0_cond_in['Wada'], 'L0_cond_bada': _L0_cond_in['bada'], 'L1_cond_ln_g': _L1_cond_in['ln_g'], 'L1_cond_ln_b': _L1_cond_in['ln_b'], 'L1_cond_Wg': _L1_cond_in['Wg'], 'L1_cond_bg': _L1_cond_in['bg'], 'L1_cond_Wb': _L1_cond_in['Wb'], 'L1_cond_bb': _L1_cond_in['bb'], 'L1_cond_Wqkv': _L1_cond_in['Wqkv'], 'L1_cond_bqkv': _L1_cond_in['bqkv'], 'L1_cond_Wp': _L1_cond_in['Wp'], 'L1_cond_bp': _L1_cond_in['bp'], 'L1_cond_W1': _L1_cond_in['W1'], 'L1_cond_b1': _L1_cond_in['b1'], 'L1_cond_W2': _L1_cond_in['W2'], 'L1_cond_b2': _L1_cond_in['b2']}

def reference(x, cond_1024, L0_cond_Wqkv, L0_cond_Wproj, L0_cond_bproj, L0_cond_W1, L0_cond_b1, L0_cond_W2, L0_cond_b2, L0_cond_g1, L0_cond_be1, L0_cond_g2, L0_cond_be2, L0_cond_Wada, L0_cond_bada, L1_cond_ln_g, L1_cond_ln_b, L1_cond_Wg, L1_cond_bg, L1_cond_Wb, L1_cond_bb, L1_cond_Wqkv, L1_cond_bqkv, L1_cond_Wp, L1_cond_bp, L1_cond_W1, L1_cond_b1, L1_cond_W2, L1_cond_b2):
    import jax
    import jax.numpy as jnp

    def _L0_cond_ref(x, condition, Wqkv, Wproj, bproj, W1, b1, W2, b2, g1, be1, g2, be2, Wada, bada):
        import jax, jax.numpy as jnp
        import numpy as np
        D = 256
        H = 16
        HD = 4 * D
        B, T = (4, 256)
        EPS = 1e-05

        def _layernorm(x, g, b):
            mu = jnp.mean(x, axis=-1, keepdims=True)
            var = jnp.mean(jnp.square(x - mu), axis=-1, keepdims=True)
            return (x - mu) * jax.lax.rsqrt(var + EPS) * g + b

        def _attention(x, Wqkv, Wproj, bproj):
            b, t, c = x.shape
            hd = c // H
            qkv = (x @ Wqkv).reshape(b, t, 3, H, hd).transpose(2, 0, 3, 1, 4)
            q, k, v = (qkv[0], qkv[1], qkv[2])
            scale = hd ** (-0.5)
            scores = jnp.einsum('bhqd,bhkd->bhqk', q, k) * scale
            causal = jnp.tril(jnp.ones((t, t), bool))
            scores = jnp.where(causal, scores, -jnp.inf)
            attn = jax.nn.softmax(scores, axis=-1)
            out = jnp.einsum('bhqk,bhkd->bhqd', attn, v)
            out = out.transpose(0, 2, 1, 3).reshape(b, t, c)
            return out @ Wproj + bproj
        mod = jax.nn.silu(condition) @ Wada + bada
        sh_a, sc_a, gt_a, sh_m, sc_m, gt_m = jnp.split(mod, 6, axis=1)
        xn = _layernorm(x, g1, be1)
        xm = xn * (1.0 + sc_a[:, None, :]) + sh_a[:, None, :]
        x = x + gt_a[:, None, :] * _attention(xm, Wqkv, Wproj, bproj)
        xn = _layernorm(x, g2, be2)
        xm = xn * (1.0 + sc_m[:, None, :]) + sh_m[:, None, :]
        h = jax.nn.gelu(xm @ W1 + b1, approximate=False)
        x = x + gt_m[:, None, :] * (h @ W2 + b2)
        return x

    def _L1_cond_ref(hidden, w, ln_g, ln_b, Wg, bg, Wb, bb, Wqkv, bqkv, Wp, bp, W1, b1, W2, b2, num_heads):
        import jax, jax.numpy as jnp
        import numpy as np
        EPS = 1e-05

        def _sln(h, w, ln_g, ln_b, Wg, bg, Wb, bb):
            mu = jnp.mean(h, axis=-1, keepdims=True)
            var = jnp.mean((h - mu) ** 2, axis=-1, keepdims=True)
            ln = (h - mu) / jnp.sqrt(var + EPS) * ln_g + ln_b
            gamma = (w @ Wg.T + bg)[:, None, :]
            beta = (w @ Wb.T + bb)[:, None, :]
            return gamma * ln + beta
        B, N, D = hidden.shape
        hd = D // num_heads
        h = _sln(hidden, w, ln_g, ln_b, Wg, bg, Wb, bb)
        qkv = (h @ Wqkv.T + bqkv).reshape(B, N, num_heads, hd, 3)
        q = jnp.moveaxis(qkv[..., 0], 2, 1)
        k = jnp.moveaxis(qkv[..., 1], 2, 1)
        v = jnp.moveaxis(qkv[..., 2], 2, 1)
        energy = jnp.einsum('bhqd,bhkd->bhqk', q, k)
        att = jax.nn.softmax(energy, axis=-1) / D ** 0.5
        out = jnp.einsum('bhqk,bhkd->bhqd', att, v)
        out = jnp.moveaxis(out, 1, 2).reshape(B, N, D)
        out = out @ Wp.T + bp
        h1 = out + hidden
        h2 = _sln(h1, w, ln_g, ln_b, Wg, bg, Wb, bb)
        return h2 + h1
    x = _L0_cond_ref(x, cond_1024, L0_cond_Wqkv, L0_cond_Wproj, L0_cond_bproj, L0_cond_W1, L0_cond_b1, L0_cond_W2, L0_cond_b2, L0_cond_g1, L0_cond_be1, L0_cond_g2, L0_cond_be2, L0_cond_Wada, L0_cond_bada)
    x = _L1_cond_ref(x, cond_1024, L1_cond_ln_g, L1_cond_ln_b, L1_cond_Wg, L1_cond_bg, L1_cond_Wb, L1_cond_bb, L1_cond_Wqkv, L1_cond_bqkv, L1_cond_Wp, L1_cond_bp, L1_cond_W1, L1_cond_b1, L1_cond_W2, L1_cond_b2, 16)
    return x

_drawn_inputs = setup_inputs


def setup_inputs(seed=0):
    import zlib

    import numpy as np

    out = dict(_drawn_inputs(seed))
    spreads = {'L0_cond_bproj': (0.0, 0.476),
     'L0_cond_b1': (0.0, 0.8),
     'L0_cond_b2': (0.0, 0.539),
     'L0_cond_g1': (1.0, 0.6),
     'L0_cond_be1': (0.0, 0.8),
     'L0_cond_g2': (1.0, 0.6),
     'L0_cond_be2': (0.0, 0.8),
     'L1_cond_ln_g': (1.0, 0.2),
     'L1_cond_ln_b': (0.0, 0.1),
     'L1_cond_bg': (0.0, 0.1),
     'L1_cond_bb': (0.0, 0.1),
     'L1_cond_bqkv': (0.0, 2.0),
     'L1_cond_bp': (0.0, 0.1),
     'L1_cond_b1': (0.0, 0.1),
     'L1_cond_b2': (0.0, 0.1)}
    factors = {'L0_cond_Wqkv': 8.0,
     'L0_cond_Wproj': 8.0,
     'L0_cond_W1': 2.945,
     'L0_cond_W2': 2.698,
     'L0_cond_bada': 8.0}
    for name, (base, spread) in spreads.items():
        noise = np.random.default_rng([zlib.crc32(name.encode()), seed]).standard_normal(out[name].shape)
        drawn = base * np.exp(spread * noise) if base else spread * noise
        out[name] = jnp.asarray(drawn.astype(out[name].dtype))
    for name, factor in factors.items():
        out[name] = (out[name] * factor).astype(out[name].dtype)
    return out
```

```python
from contextlib import ExitStack

import concourse.bass as bass
import numpy as np
from concourse import mybir

F32 = mybir.dt.float32
BF16 = mybir.dt.bfloat16
ALU = mybir.AluOpType
ACT = mybir.ActivationFunctionType
AX = mybir.AxisListType

P = 128
B, T, D = 8, 512, 256
H = 16
HD = D // H
F = 4 * D
EPS = 1e-5
TT = T // P
KT = D // P
FT = F // P
GROUPS = H // 4
CUTS = 6
CUT_ROWS = CUTS * HD
ALL_ROWS = CUT_ROWS + 3
Q_PARTS = (0, 0, 0, 1, 1, 2)
K_PARTS = (0, 1, 2, 0, 1, 0)
VW = HD + 1
VROW = H * VW + 16
STEPS = GROUPS * TT
MASKED = -3.0e38
GATE_A, GATE_A_BIAS, GATE_M, GATE_M_BIAS, NORM1, SHIFT1, NORM_A, SHIFT_A, NORM_M, SHIFT_M = range(10)
BY_FEATURE = (NORM_A, SHIFT_A, NORM_M, SHIFT_M, NORM1, SHIFT1)

SLOT_X = {0: ("hold1", "sums0"), 3: ("proj0",), 4: ("norm_m",), 6: ("turn_m",), 7: ("up_a",),
          8: ("up_b",), 9: ("down_a",), 10: ("down_b",), 11: ("keep0", "norm_1"), 12: ("turn_1",),
          13: ("q1",), 14: ("k1",)}
AFTER_X = ("v1", "max0", "stack1")
SLOT_Y = {0: ("sums1",), 3: ("proj1",), 4: ("norm_o",), 5: ("close1", "norm_a"), 7: ("turn_a",),
          9: ("q0",), 10: ("k0",)}
AFTER_Y = ("v0", "max1", "stack0")
BEHIND = {"hold1": 2, "sums0": 1, "proj0": 1, "norm_m": 1, "turn_m": 1, "up_a": 1, "up_b": 1,
          "down_a": 1, "down_b": 1, "keep0": 0, "norm_1": 1, "turn_1": 1, "q1": 1, "k1": 1,
          "v1": 1, "stack1": 1, "max0": 0, "sums1": 2, "proj1": 2, "norm_o": 2, "close1": 2,
          "norm_a": -1, "turn_a": -1, "q0": -1, "k0": -1, "v0": -1, "stack0": -1, "max1": 1}
SCAN_Y = [()] * 3 + [(h,) for h in range(10)] + [(10, 11), (12, 13), (14, 15)]
FIRST = ("norm_a", "turn_a", "q0", "k0", "v0", "stack0")
ADDS = {"proj0": {"dense": 2, "gated_a": 1}, "proj1": {"dense": 2}, "down_a": {"dense": 1},
        "down_b": {"dense": 1, "gated_m": 1}, "up_a": {"dense": 4}, "up_b": {"dense": 4},
        "max0": {"dense": 1, "maxima": 1, "max0": 1}, "max1": {"dense": 1, "maxima": 1, "max1": 1},
        "hold1": {"hold": 1}, "sums0": {"sums": 1, "rows0": 1}, "sums1": {"sums": 1, "rows1": 1},
        "keep0": {"keep": 1, "x_in": 1}, "close1": {"close": 1},
        "stack0": {"stack0": 1}, "stack1": {"stack1": 1}}
for _n in ("turn_m", "turn_1", "turn_a", "v0", "v1"):
    ADDS[_n] = {"dense": 2}
for _n in ("q0", "k0", "q1", "k1"):
    ADDS[_n] = {"dense": 2, "cut": 1}
for _n in ("norm_m", "norm_1", "norm_a", "norm_o"):
    ADDS[_n] = {"norm": 1}
COUNTS = ("dense", "gated_a", "gated_m", "maxima", "max0", "max1", "hold", "sums", "rows0", "rows1",
          "keep", "x_in", "close", "stack0", "stack1", "cut", "norm", "head", "step", "group",
          "scan")


class Loop:

    def __init__(self, eng, i, passed):
        self.eng, self.i, self.passed, self.registers = eng, i, passed, {}

    def apart(self):
        self.eng.sem_inc(self.passed, 1)

    def value(self, per, fixed):
        if per not in self.registers:
            pair = self.eng.alloc_register(f"grown_{per}"), self.eng.alloc_register(f"value_{per}")
            self.registers[per] = pair
            self.apart()
            self.eng.reg_mul(pair[0], self.i, per)
        grown, value = self.registers[per]
        if not fixed:
            return grown
        self.eng.reg_add(value, grown, fixed)
        return value


class Count:

    def __init__(self):
        self.n, self.start, self.loop, self.per = 0, 0, None, 0

    def enter(self, loop, first, per):
        self.start, self.n, self.loop, self.first, self.per = self.n, 0, loop, first, per

    def leave(self, passes):
        assert self.n == self.per, (self.n, self.per)
        self.n, self.loop = self.start + passes * self.per, None

    def at(self, times=1, add=0):
        if self.loop is None:
            return self.n * times + add
        fixed = (self.start - self.first * self.per + self.n) * times + add
        return self.loop, self.per * times, fixed

    def index(self):
        return self.n if self.loop is None else self.start + self.n


def per_pass():
    per = dict.fromkeys(COUNTS, 0)
    for slot in (*SLOT_X.values(), AFTER_X, *SLOT_Y.values(), AFTER_Y):
        for chunk in slot:
            for name, n in ADDS[chunk].items():
                per[name] += n
    per.update(head=2 * 4 * STEPS, step=2 * STEPS, group=2 * GROUPS, scan=2 * H * TT)
    return per


PER = per_pass()
FIRST_FULL, LAST_FULL = 3, B - 2


def wait(eng, sem, value, apart=False):
    if isinstance(value, int):
        if value > 0:
            eng.wait_ge(sem, value)
        return
    loop, per, fixed = value
    assert FIRST_FULL * per + fixed > 0, (per, fixed)
    eng.wait_ge(sem, loop.value(per, fixed))
    if apart:
        loop.apart()


def run_passes(eng, work, passed):
    at = {name: Count() for name in COUNTS}
    at["x_in"].n = 1
    for chunk in FIRST:
        do_chunk(at, work, chunk, 0)
    for i in range(FIRST_FULL):
        one_pass(at, work, i, i)
    with eng.Fori(FIRST_FULL, LAST_FULL + 1) as i:
        loop = Loop(eng, i, passed)
        for name in COUNTS:
            at[name].enter(loop, FIRST_FULL, PER[name])
        one_pass(at, work, i, None)
    for name in COUNTS:
        at[name].leave(LAST_FULL + 1 - FIRST_FULL)
    for i in range(LAST_FULL + 1, B + 2):
        one_pass(at, work, i, i)
    return at


def do_chunk(at, work, chunk, b):
    work(at, "chunk", chunk, b)
    for name, n in ADDS[chunk].items():
        at[name].n += n


def one_pass(at, work, i, number):

    def live(behind):
        return number is None or 0 <= number - behind < B

    for slot, after, attend, scan, heads in (
        (SLOT_X, AFTER_X, 1, 0, [(h,) for h in range(H)]),
        (SLOT_Y, AFTER_Y, 0, 1, SCAN_Y),
    ):
        attending = live(2 if attend else 0)
        scanning = live(1 if scan else 0)
        for s in range(STEPS):
            work(at, "step", (s, attend if attending else None, scan, heads[s] if scanning else ()), i)
            if attending:
                at["head"].n += 4
                at["step"].n += 1
                at["group"].n += s > 0 and s % TT == 0
            at["scan"].n += TT * len(heads[s]) if scanning else 0
            for chunk in slot.get(s, ()):
                if live(BEHIND[chunk]):
                    do_chunk(at, work, chunk, i - BEHIND[chunk])
        if attending:
            work(at, "last", attend, i)
            at["group"].n += 1
        for chunk in after:
            if live(BEHIND[chunk]):
                do_chunk(at, work, chunk, i - BEHIND[chunk])


def two_layers(nc, x, cond_t, wqkv0, wproj0, w1, w2, wada, wqkv1, wp1, wgb1, b1, b_qk1, bv1, bp1,
               vectors, out):
    ctx = ExitStack()
    with ctx:
        def sb(name, shape, dt=F32):
            return ctx.enter_context(nc.sbuf_tensor(name, shape, dt))

        def pb(name, shape, dt=F32):
            return ctx.enter_context(nc.psum_tensor(name, shape, dt))

        def sem(name):
            return ctx.enter_context(nc.semaphore(name))

        WQKV = [sb("WQKV0", [P, KT, 3 * D]), sb("WQKV1", [P, KT, 3 * D])]
        WP = [sb("WP0", [P, KT, D]), sb("WP1", [P, KT, D])]
        W1 = sb("W1", [P, KT, F])
        W2 = sb("W2", [P, FT, D])
        B1 = sb("B1", [P, FT])
        BQK1 = sb("BQK1", [P, 4])
        BV1 = sb("BV1", [P, D])
        BP1 = sb("BP1", [P, D])
        QS = [sb("QS0", [P, H, T], BF16), sb("QS1", [P, H, T], BF16)]
        KS = [sb("KS0", [P, H, T], BF16), sb("KS1", [P, H, T], BF16)]
        V = [sb("V0", [P, TT, VROW]), sb("V1", [P, TT, VROW])]
        E = sb("E", [P, 2, 4, T])
        HID = sb("HID", [P, FT, T])
        OE = sb("OE", [P, GROUPS, T])
        OC = sb("OC", [P, KT, T])
        RB = sb("RB", [P, KT, T])
        RS = sb("RS", [P, T // 8])
        RR = sb("RR", [P, T // 8])
        XIN = sb("XIN", [P, TT, D])
        XR = sb("XR", [P, TT, D])
        R1 = sb("R1", [P, TT, D])
        RH = sb("RH", [P, TT, D])
        TMP = sb("TMP", [P, TT, D])
        XN = sb("XN", [P, TT, D])
        OUT = sb("OUT", [P, TT, D])
        XT = sb("XT", [P, KT, T])
        X32 = sb("X32", [P, 2, T])
        PART = sb("PART", [P, 2, 3, 2, T], BF16)
        ROW0 = sb("ROW0", [P, 4, D])
        ROW1 = sb("ROW1", [P, 2, D])
        NT = sb("NT", [3 * H, T], BF16)
        MX = sb("MX", [P, TT, H])
        MR = sb("MR", [P, TT, H])
        NMP = sb("NMP", [P, TT, 3, H], BF16)
        STAT = sb("STAT", [P, TT, 6])
        MV = sb("MV", [P, TT, 2])
        VE = sb("VE", [P, TT])
        RSTD = sb("RSTD", [P, TT])
        HALF = sb("HALF", [P, TT])
        FM = sb("FM", [P, len(BY_FEATURE) * KT, B])
        ID32 = sb("ID32", [P, P])
        ID16 = sb("ID16", [P, P], BF16)
        CAUSAL = sb("CAUSAL", [P, P], BF16)
        CAUSAL_T = sb("CAUSAL_T", [P, P], BF16)
        CT = sb("CT", [P, KT, B])
        CE = sb("CE", [P, KT, B])
        CS = sb("CS", [P, KT, B])
        WADA = HID[:, 0:6, :].rearrange("p a b -> p (a b)").rearrange("p (k n) -> p k n", k=KT)
        WGB = E[:, 0, 0:2, :]
        MODS = OE[0:B, 0:3, :].rearrange("p a b -> p (a b)")
        GB = OE[0:B, 3, :]
        ROWS = QS[0].bitcast(F32)[0:B, 0:10, :]
        VEC = QS[1].bitcast(F32)[0:B, :, :].rearrange("p a b -> p (a b)")

        SC = [pb(f"SC{i}", [P, T]) for i in range(3)]
        DN = [pb(f"DN{i}", [P, T]) for i in range(2)]
        SX = [pb(f"SX{i}", [P, T]) for i in range(2)]
        OP = pb("OP", [P, T])

        sums_dram = nc.dram_tensor("recip_sums", (4, GROUPS, T), F32, kind="Internal").ap()
        rows_dram = nc.dram_tensor("row_vectors", (B, 6, D), F32, kind="Internal").ap()

        first_load = sem("first_load")
        other_load = sem("other_load")
        consts = sem("consts")
        set_act = sem("set_act")
        set_dve = sem("set_dve")
        set_pe = sem("set_pe")
        rows_out = sem("rows_out")
        x_dma = sem("x_dma")
        dense_full = sem("dense_full")
        dense_done = sem("dense_done")
        head_full = sem("head_full")
        exp_done = sem("exp_done")
        scan_full = sem("scan_full")
        scan_done = sem("scan_done")
        pv_done = sem("pv_done")
        out_done = sem("out_done")
        stat_dve = sem("stat_dve")
        norm_pool = sem("norm_pool")
        high_dve = sem("high_dve")
        cut_pool = sem("cut_pool")
        max_pool = sem("max_pool")
        max_dma = [sem("max_dma0"), sem("max_dma1")]
        stack_dma = [sem("stack_dma0"), sem("stack_dma1")]
        compact_dma = sem("compact_dma")
        recip_dve = sem("recip_dve")
        recip_dma = sem("recip_dma")
        spread_dma = sem("spread_dma")
        scaled_pool = sem("scaled_pool")
        row0_dma = sem("row0_dma")
        row1_dma = sem("row1_dma")
        res_a_pool = sem("res_a_pool")
        res_m_pool = sem("res_m_pool")
        hold_pool = sem("hold_pool")
        keep_dve = sem("keep_dve")
        close_pool = sem("close_pool")
        store_dma = sem("store_dma")

        passed = {name: sem(f"passed_{name}") for name in ("sp", "pool", "act", "dve", "pe")}

        block = ctx.enter_context(nc.Block())

        @block.sync
        def _(sp):
            sp.dma_start(CT[:], cond_t.rearrange("(k p) b -> p k b", p=P)).then_inc(first_load, 16)
            sp.dma_start(WADA, wada.rearrange("(k p) n -> p k n", p=P)).then_inc(first_load, 16)
            sp.dma_start(WGB, wgb1.rearrange("(k p) n -> p k n", p=P)).then_inc(first_load, 16)
            at_col = 0
            for v in vectors:
                n = v.shape[0]
                sp.dma_start(VEC[:, at_col:at_col + n],
                             v.unsqueeze(0).to_broadcast([B, n])).then_inc(first_load, 16)
                at_col += n
            sp.dma_start(WQKV[0][:], wqkv0.rearrange("(k p) n -> p k n", p=P)).then_inc(first_load, 16)
            sp.dma_start(WP[0][:], wproj0.rearrange("(k p) n -> p k n", p=P)).then_inc(first_load, 16)
            sp.dma_start(XIN[:], x[0].rearrange("(t p) d -> p t d", p=P)).then_inc(x_dma, 16)
            sp.dma_start(W1[:], w1.rearrange("(k p) n -> p k n", p=P)).then_inc(other_load, 16)
            sp.dma_start(W2[:], w2.rearrange("(k p) n -> p k n", p=P)).then_inc(other_load, 16)
            sp.dma_start(WQKV[1][:], wqkv1.rearrange("(k p) n -> p k n", p=P)).then_inc(other_load, 16)
            sp.dma_start(WP[1][:], wp1.rearrange("(k p) n -> p k n", p=P)).then_inc(other_load, 16)
            with nc.allow_non_contiguous_dma(reason="small bias vectors by feature"):
                sp.dma_start(B1[:], b1.rearrange("(k p) -> p k", p=P)).then_inc(other_load, 16)
                sp.dma_start(BQK1[:], b_qk1.rearrange("(k p) -> p k", p=P)).then_inc(other_load, 16)
            sp.dma_start(BV1[:], bv1.unsqueeze(0).to_broadcast([P, D])).then_inc(other_load, 16)
            sp.dma_start(BP1[:], bp1.unsqueeze(0).to_broadcast([P, D])).then_inc(other_load, 16)
            sp.wait_ge(set_dve, ROWS_READY)
            sp.dma_start(rows_dram, ROWS[:, 0:6, :]).then_inc(rows_out, 16)
            sp.wait_ge(rows_out, 16)

            def work(at, kind, what, b):
                if kind != "chunk":
                    return
                if what in ("sums0", "sums1"):
                    if what == "sums0":
                        wait(sp, res_m_pool, at["gated_m"].at(2), apart=True)
                        wait(sp, dense_done, at["dense"].at(), apart=True)
                        sp.dma_start(ROW0[:], rows_dram[bass.ds(b, 1), 0:4, :].to_broadcast([P, 4, D]))\
                            .then_inc(row0_dma, 16)
                    else:
                        wait(sp, close_pool, at["close"].at(3), apart=True)
                        sp.dma_start(ROW1[:], rows_dram[bass.ds(b, 1), 4:6, :].to_broadcast([P, 2, D]))\
                            .then_inc(row1_dma, 16)
                    wait(sp, out_done, at["group"].at(), apart=True)
                    wait(sp, dense_full, at["dense"].at(), apart=True)
                    wait(sp, recip_dve, at["sums"].at(), apart=True)
                    for j in range(4):
                        sp.dma_start(OC[64 * (j % 2):64 * (j % 2) + 64, j // 2, :],
                                     OE[32 * j:32 * j + HD, :, :]).then_inc(compact_dma, 16)
                    sp.dma_start(RS[:], OE[HD:P:32, :, :]).then_inc(compact_dma, 16)
                    wait(sp, recip_dve, at["sums"].at(1, 1), apart=True)
                    wait(sp, spread_dma, at["sums"].at(64), apart=True)
                    sp.dma_start(sums_dram.rearrange("j g (c n) -> (j g c) n", c=8), RR[:])\
                        .then_inc(recip_dma, 16)
                    wait(sp, recip_dma, at["sums"].at(16, 16), apart=True)
                    wait(sp, scaled_pool, at["sums"].at(), apart=True)
                    for j in range(4):
                        sp.dma_start(RB[64 * (j % 2):64 * (j % 2) + 64, j // 2, :],
                                     sums_dram[j].unsqueeze(0).to_broadcast([HD, GROUPS, T]))\
                            .then_inc(spread_dma, 16)
                elif what == "keep0":
                    wait(sp, keep_dve, at["keep"].at(1, 1), apart=True)
                    wait(sp, norm_pool, at["norm"].at(6), apart=True)
                    if not isinstance(b, int) or b + 1 < B:
                        sp.dma_start(XIN[:], x[bass.ds(b + 1, 1)].rearrange("a (t p) d -> p (a t) d", p=P))\
                            .then_inc(x_dma, 16)
                elif what == "close1":
                    wait(sp, close_pool, at["close"].at(3, 3), apart=True)
                    sp.dma_start(out[bass.ds(b, 1)].rearrange("a (t p) d -> p (a t) d", p=P), OUT[:])\
                        .then_inc(store_dma, 16)
                elif what in ("stack0", "stack1"):
                    n = int(what[-1])
                    wait(sp, high_dve, at["cut"].at(), apart=True)
                    wait(sp, cut_pool, at["cut"].at(3), apart=True)
                    wait(sp, pv_done, at["step"].at(), apart=True)
                    for r in range(CUTS):
                        sp.dma_start(QS[n][HD * r:HD * r + HD, :, :], PART[:, 0, Q_PARTS[r], :, :])\
                            .then_inc(stack_dma[n], 16)
                        sp.dma_start(KS[n][HD * r:HD * r + HD, :, :], PART[:, 1, K_PARTS[r], :, :])\
                            .then_inc(stack_dma[n], 16)

            run_passes(sp, work, passed["sp"])
            sp.wait_ge(store_dma, 16 * B)

        @block.gpsimd
        def _(pool):
            g = nc.gpsimd
            g.memset(ID32[:], 0.0).then_inc(consts, 1)
            g.memset(ID16[:], 0.0).then_inc(consts, 1)
            g.memset(CAUSAL[:], 0.0).then_inc(consts, 1)
            g.memset(CAUSAL_T[:], 0.0).then_inc(consts, 1)
            pool.wait_ge(consts, 4)
            for m in (ID32, ID16):
                g.affine_select(out=m[:], in_=m[:], compare_op=ALU.not_equal, fill=1.0, base=0,
                                pattern=[[-1, P]], channel_multiplier=1).then_inc(consts, 1)
            g.affine_select(out=CAUSAL[:], in_=CAUSAL[:], compare_op=ALU.is_ge, fill=MASKED, base=0,
                            pattern=[[-1, P]], channel_multiplier=1).then_inc(consts, 1)
            g.affine_select(out=CAUSAL_T[:], in_=CAUSAL_T[:], compare_op=ALU.is_ge, fill=MASKED, base=0,
                            pattern=[[1, P]], channel_multiplier=-1).then_inc(consts, 1)
            g.memset(HALF[:], -0.5).then_inc(consts, 1)
            g.memset(V[0][:], 1.0).then_inc(consts, 1)
            g.memset(V[1][:], float(D) ** 0.5).then_inc(consts, 1)
            pool.wait_ge(consts, N_CONSTS - 2)
            g.memset(KS[0][CUT_ROWS:ALL_ROWS, :, :], 1.0).then_inc(consts, 1)
            pool.wait_ge(consts, N_CONSTS - 1)
            g.memset(KS[1][CUT_ROWS:ALL_ROWS, :, :], 1.0).then_inc(consts, 1)
            pool.wait_ge(consts, N_CONSTS)

            def norm(at, src):
                wait(pool, stat_dve, at["norm"].at(8, 8), apart=True)
                wait(pool, dense_full, at["dense"].at(), apart=True)
                wait(pool, close_pool, at["close"].at(3), apart=True)
                wait(pool, norm_pool, at["norm"].at(6), apart=True)
                g.tensor_scalar(VE[:], MV[:, :, 1], 1.0, EPS, ALU.mult, ALU.add).then_inc(norm_pool, 1)
                wait(pool, norm_pool, at["norm"].at(6, 1), apart=True)
                g.tensor_tensor(RSTD[:], VE[:], HALF[:], ALU.pow).then_inc(norm_pool, 1)
                wait(pool, norm_pool, at["norm"].at(6, 2), apart=True)
                for t in range(TT):
                    g.tensor_scalar(XN[:, t, :], src[:, t, :], MV[:, t, 0:1], RSTD[:, t:t + 1],
                                    ALU.subtract, ALU.mult).then_inc(norm_pool, 1)

            def work(at, kind, what, b):
                if kind != "chunk":
                    return
                if what in ("norm_a", "norm_m", "norm_1", "norm_o"):
                    src = {"norm_a": XIN, "norm_m": XR, "norm_1": R1, "norm_o": TMP}[what]
                    if what == "norm_a":
                        wait(pool, x_dma, at["x_in"].at(16), apart=True)
                    if what == "norm_o":
                        wait(pool, dense_done, at["dense"].at(), apart=True)
                    norm(at, src)
                elif what in ("q0", "k0", "q1", "k1"):
                    side = "qk".index(what[0])
                    part = PART[:, side, :, :, :]
                    c = at["cut"]
                    wait(pool, high_dve, c.at(1, 1), apart=True)
                    wait(pool, stack_dma[0], at["stack0"].at(192), apart=True)
                    wait(pool, stack_dma[1], at["stack1"].at(192), apart=True)
                    g.tensor_tensor(X32[:], X32[:], part[:, 0], ALU.subtract).then_inc(cut_pool, 1)
                    wait(pool, cut_pool, c.at(3, 1), apart=True)
                    g.tensor_scalar(part[:, 1], X32[:], 1.0, 0.0, ALU.mult, ALU.add).then_inc(cut_pool, 1)
                    wait(pool, cut_pool, c.at(3, 2), apart=True)
                    g.tensor_tensor(part[:, 2], X32[:], part[:, 1], ALU.subtract).then_inc(cut_pool, 1)
                elif what in ("max0", "max1"):
                    m = at["maxima"]
                    wait(pool, scan_done, at["scan"].at(), apart=True)
                    wait(pool, dense_full, at["dense"].at(), apart=True)
                    g.tensor_scalar(NMP[:, :, 0, :], MX[:], 1.0, 0.0, ALU.mult, ALU.add).then_inc(max_pool, 1)
                    wait(pool, max_pool, m.at(4, 1), apart=True)
                    g.tensor_tensor(MR[:], MX[:], NMP[:, :, 0, :], ALU.subtract).then_inc(max_pool, 1)
                    wait(pool, max_pool, m.at(4, 2), apart=True)
                    g.tensor_scalar(NMP[:, :, 1, :], MR[:], 1.0, 0.0, ALU.mult, ALU.add).then_inc(max_pool, 1)
                    wait(pool, max_pool, m.at(4, 3), apart=True)
                    g.tensor_tensor(NMP[:, :, 2, :], MR[:], NMP[:, :, 1, :], ALU.subtract).then_inc(max_pool, 1)
                elif what in ("sums0", "sums1"):
                    wait(pool, spread_dma, at["sums"].at(64, 64), apart=True)
                    wait(pool, compact_dma, at["sums"].at(80, 80), apart=True)
                    g.tensor_tensor(OC[:], OC[:], RB[:], ALU.mult).then_inc(scaled_pool, 1)
                elif what == "proj0":
                    c = at["gated_a"]
                    wait(pool, row0_dma, at["rows0"].at(16), apart=True)
                    wait(pool, keep_dve, at["keep"].at(), apart=True)
                    g.tensor_tensor(XR[:], XR[:], ROW0[:, 1:2, :].to_broadcast([P, TT, D]), ALU.add)\
                        .then_inc(res_a_pool, 1)
                    wait(pool, res_a_pool, c.at(2, 1), apart=True)
                    wait(pool, dense_done, at["dense"].at(1, 2), apart=True)
                    g.tensor_tensor(XR[:], XR[:], TMP[:], ALU.add).then_inc(res_a_pool, 1)
                elif what == "down_b":
                    c = at["gated_m"]
                    wait(pool, norm_pool, at["norm"].at(6), apart=True)
                    wait(pool, hold_pool, at["hold"].at(), apart=True)
                    g.tensor_tensor(XR[:], XR[:], ROW0[:, 3:4, :].to_broadcast([P, TT, D]), ALU.add)\
                        .then_inc(res_m_pool, 1)
                    wait(pool, res_m_pool, c.at(2, 1), apart=True)
                    wait(pool, dense_done, at["dense"].at(1, 1), apart=True)
                    g.tensor_tensor(R1[:], XR[:], TMP[:], ALU.add).then_inc(res_m_pool, 1)
                elif what == "hold1":
                    wait(pool, res_m_pool, at["gated_m"].at(2), apart=True)
                    wait(pool, other_load, 16 * N_LOAD, apart=True)
                    wait(pool, dense_done, at["dense"].at(), apart=True)
                    g.tensor_tensor(RH[:], R1[:], BP1[:].unsqueeze(1).to_broadcast([P, TT, D]), ALU.add)\
                        .then_inc(hold_pool, 1)
                elif what == "close1":
                    c = at["close"]
                    wait(pool, norm_pool, at["norm"].at(6), apart=True)
                    wait(pool, row1_dma, at["rows1"].at(16), apart=True)
                    wait(pool, store_dma, c.at(16), apart=True)
                    g.tensor_tensor(XN[:], XN[:], ROW1[:, 0:1, :].to_broadcast([P, TT, D]), ALU.mult)\
                        .then_inc(close_pool, 1)
                    g.tensor_tensor(TMP[:], TMP[:], ROW1[:, 1:2, :].to_broadcast([P, TT, D]), ALU.add)\
                        .then_inc(close_pool, 1)
                    wait(pool, close_pool, c.at(3, 2), apart=True)
                    g.tensor_tensor(OUT[:], XN[:], TMP[:], ALU.add).then_inc(close_pool, 1)

            run_passes(pool, work, passed["pool"])

        @block.scalar
        def _(act):
            a = nc.scalar
            act.wait_ge(first_load, 16 * N_FIRST_LOAD)
            a.activation(CE[:], CT[:], ACT.Exp, scale=-1.0).then_inc(set_act, 1)
            act.wait_ge(other_load, 16 * N_LOAD)
            act.wait_ge(set_dve, FM_READY)

            def work(at, kind, what, b):
                if kind == "step":
                    s, attend, _, _ = what
                    if attend is None:
                        return
                    lo = P * (s % TT) if attend == 0 else 0
                    for j in range(4):
                        if j == 0:
                            wait(act, pv_done, at["step"].at(1, -1))
                        wait(act, head_full, at["head"].at(1, j + 1))
                        a.activation(E[:, at["step"].index() % 2, j, lo:T], SC[(4 * s + j) % 3][:, lo:T],
                                     ACT.Exp, scale=HD ** -0.5 if attend == 0 else 1.0)\
                            .then_inc(exp_done, 1)
                    return
                if kind != "chunk":
                    return
                c = at["dense"]

                def bank(k):
                    wait(act, dense_full, c.at(1, k + 1))
                    return DN[(c.index() + k) % 2]

                if what in ("turn_a", "turn_m", "turn_1"):
                    first = {"turn_a": 0, "turn_m": 2, "turn_1": 4}[what]
                    for ft in range(KT):
                        a.activation(XT[:, ft, :], bank(ft)[:], ACT.Identity,
                                     scale=FM[:, first * KT + ft, bass.ds(b, 1)],
                                     bias=FM[:, (first + 1) * KT + ft, bass.ds(b, 1)])\
                            .then_inc(dense_done, 1)
                elif what in ("q0", "k0", "q1", "k1"):
                    side = "qk".index(what[0])
                    wait(act, cut_pool, at["cut"].at(3))
                    wait(act, high_dve, at["cut"].at())
                    for t in range(2):
                        if what[1] == "0":
                            ins = a.activation(X32[:, t, :], bank(t)[:], ACT.Copy)
                        else:
                            ins = a.activation(X32[:, t, :], bank(t)[:], ACT.Identity,
                                               bias=BQK1[:, 2 * side + t:2 * side + t + 1])
                        ins.then_inc(dense_done, 1)
                elif what in ("up_a", "up_b"):
                    for k in range(4):
                        ht = k + 4 * (what == "up_b")
                        a.activation(HID[:, ht, :], bank(k)[:], ACT.Gelu, bias=B1[:, ht:ht + 1])\
                            .then_inc(dense_done, 1)
                elif what in ("max0", "max1"):
                    n = int(what[-1])
                    psum = bank(0)
                    wait(act, max_dma[0], at["max0"].at(16))
                    wait(act, max_dma[1], at["max1"].at(16))
                    a.activation(NT[:], psum.bitcast(BF16)[0:3 * H, 0:T], ACT.Copy).then_inc(dense_done, 1)
                    wait(act, dense_done, c.at(1, 1))
                    wait(act, pv_done, at["step"].at())
                    act.dma_start(QS[n][CUT_ROWS:ALL_ROWS, :, :], NT[:]).then_inc(max_dma[n], 16)

            run_passes(act, work, passed["act"])

        @block.vector
        def _(dve):
            v = nc.vector
            done = [0]

            def then(ins):
                done[0] += 1
                ins.then_inc(set_dve, 1)
                return done[0]

            dve.wait_ge(set_act, 1)
            n = then(v.tensor_scalar(CE[:], CE[:], 1.0, 1.0, ALU.mult, ALU.add))
            dve.wait_ge(set_dve, n)
            n = then(v.reciprocal(CE[:], CE[:]))
            dve.wait_ge(set_dve, n)
            n = then(v.tensor_tensor(CS[:], CT[:], CE[:], ALU.mult))
            assert n == SILU_READY
            dve.wait_ge(first_load, 16 * N_FIRST_LOAD)
            for c in range(3):
                dve.wait_ge(set_pe, c + 1)
                then(v.tensor_tensor(MODS[:, c * T:c * T + T], SC[c][0:B, :], VEC[:, c * T:c * T + T], ALU.add))
            dve.wait_ge(set_pe, 4)
            n = then(v.tensor_tensor(GB, OP[0:B, :], VEC[:, 6 * D + 8 * D:6 * D + 10 * D], ALU.add))
            dve.wait_ge(set_dve, n)

            def mod(k):
                return MODS[:, k * D:k * D + D]

            def vec(k):
                return VEC[:, (6 + k) * D:(7 + k) * D]

            (bproj, b2, g1, be1, g2, be2, ln_g, ln_b) = (vec(k) for k in range(8))
            (shift_a, scale_a, gate_a, shift_m, scale_m, gate_m) = (mod(k) for k in range(6))
            gamma, beta = GB[:, 0:D], GB[:, D:2 * D]
            then(v.tensor_copy(ROWS[:, GATE_A, :], gate_a))
            then(v.tensor_tensor(ROWS[:, GATE_A_BIAS, :], gate_a, bproj, ALU.mult))
            then(v.tensor_copy(ROWS[:, GATE_M, :], gate_m))
            then(v.tensor_tensor(ROWS[:, GATE_M_BIAS, :], gate_m, b2, ALU.mult))
            then(v.tensor_tensor(ROWS[:, NORM1, :], gamma, ln_g, ALU.mult))
            then(v.tensor_tensor(ROWS[:, SHIFT1, :], gamma, ln_b, ALU.mult))
            then(v.scalar_tensor_tensor(ROWS[:, NORM_A, :], scale_a, 1.0, g1, ALU.add, ALU.mult))
            then(v.scalar_tensor_tensor(ROWS[:, SHIFT_A, :], scale_a, 1.0, be1, ALU.add, ALU.mult))
            then(v.scalar_tensor_tensor(ROWS[:, NORM_M, :], scale_m, 1.0, g2, ALU.add, ALU.mult))
            n = then(v.scalar_tensor_tensor(ROWS[:, SHIFT_M, :], scale_m, 1.0, be2, ALU.add, ALU.mult))
            dve.wait_ge(set_dve, n)
            for row, plus in ((SHIFT1, beta), (SHIFT_A, shift_a), (SHIFT_M, shift_m)):
                n = then(v.tensor_tensor(ROWS[:, row, :], ROWS[:, row, :], plus, ALU.add))
            assert n == ROWS_READY
            dve.wait_ge(set_pe, 5)
            n = then(v.tensor_copy(FM[:], SX[0][:, 0:len(BY_FEATURE) * KT * B]
                                   .rearrange("p (k b) -> p k b", b=B)))
            assert n == FM_READY
            dve.wait_ge(set_dve, n)
            dve.wait_ge(consts, N_CONSTS)
            dve.wait_ge(other_load, 16 * N_LOAD)

            def scan(at, k, scan_head, qt):
                wait(dve, scan_full, at["scan"].at(1, k + 1))
                w = (qt + 1) * P if scan_head[0] == 0 else T
                v.reduce_max(MX[:, qt, scan_head[1]:scan_head[1] + 1],
                             SX[(at["scan"].index() + k) % 2][:, 0:w], AX.X, negate=True)\
                    .then_inc(scan_done, 1)

            def take_out(at, g):
                wait(dve, pv_done, at["step"].at())
                wait(dve, compact_dma, at["sums"].at(80))
                v.tensor_copy(OE[:, g, :], OP[:]).then_inc(out_done, 1)

            def norm(at, src):
                c = at["norm"]
                wait(dve, norm_pool, c.at(6))
                for t in range(TT):
                    v.bn_stats(STAT[:, t, :], src[:, t, :]).then_inc(stat_dve, 1)
                wait(dve, stat_dve, c.at(8, 4), apart=True)
                for t in range(TT):
                    v.bn_aggr(MV[:, t, :], STAT[:, t, :]).then_inc(stat_dve, 1)

            def work(at, kind, what, b):
                if kind == "step":
                    s, attend, layer, heads = what
                    if s == 0:
                        wait(dve, max_pool, at["maxima"].at(4))
                    out_now = attend is not None and s > 0 and s % TT == 0
                    if heads:
                        scan(at, 0, (layer, heads[0]), 0)
                        scan(at, 1, (layer, heads[0]), 1)
                    if out_now:
                        take_out(at, s // TT - 1)
                    if heads:
                        scan(at, 2, (layer, heads[0]), 2)
                        scan(at, 3, (layer, heads[0]), 3)
                    for n, h in enumerate(heads[1:]):
                        for qt in range(TT):
                            scan(at, TT * (n + 1) + qt, (layer, h), qt)
                    return
                if kind == "last":
                    take_out(at, GROUPS - 1)
                    return
                c = at["dense"]

                def bank(k):
                    wait(dve, dense_full, c.at(1, k + 1))
                    return DN[(c.index() + k) % 2]

                if what in ("norm_a", "norm_m", "norm_1", "norm_o"):
                    if what == "norm_a":
                        wait(dve, x_dma, at["x_in"].at(16))
                    if what == "norm_m":
                        wait(dve, res_a_pool, at["gated_a"].at(2))
                    if what == "norm_1":
                        wait(dve, res_m_pool, at["gated_m"].at(2))
                    if what == "norm_o":
                        wait(dve, dense_done, c.at())
                    norm(at, {"norm_a": XIN, "norm_m": XR, "norm_1": R1, "norm_o": TMP}[what])
                elif what in ("q0", "k0", "q1", "k1"):
                    side = "qk".index(what[0])
                    wait(dve, dense_done, c.at(1, 2))
                    wait(dve, stack_dma[0], at["stack0"].at(192))
                    wait(dve, stack_dma[1], at["stack1"].at(192))
                    v.tensor_copy(PART[:, side, 0, :, :], X32[:]).then_inc(high_dve, 1)
                elif what in ("v0", "v1"):
                    n = int(what[-1])
                    wait(dve, pv_done, at["step"].at())
                    for tp in range(2):
                        psum = bank(tp)[:].rearrange("p (t h d) -> p t h d", t=2, d=HD)
                        for t in range(2):
                            dst = V[n][:, 2 * tp + t, 0:H * VW].rearrange("p (h e) -> p h e", e=VW)[:, :, 0:HD]
                            if n == 0:
                                ins = v.tensor_copy(dst, psum[:, t])
                            else:
                                ins = v.tensor_tensor(dst, psum[:, t],
                                                      BV1[:].rearrange("p (h d) -> p h d", d=HD), ALU.add)
                        ins.then_inc(dense_done, 1)
                elif what == "proj0":
                    wait(dve, row0_dma, at["rows0"].at(16))
                    wait(dve, close_pool, at["close"].at(3))
                    wait(dve, res_m_pool, at["gated_m"].at(2))
                    for tp in range(2):
                        v.tensor_tensor(TMP[:, 2 * tp:2 * tp + 2, :], bank(tp)[:].rearrange("p (t d) -> p t d", d=D),
                                        ROW0[:, 0:1, :].to_broadcast([P, 2, D]), ALU.mult).then_inc(dense_done, 1)
                elif what in ("down_a", "down_b"):
                    tp = "ab".index(what[-1])
                    wait(dve, res_a_pool, at["gated_a"].at(2))
                    v.tensor_tensor(TMP[:, 2 * tp:2 * tp + 2, :], bank(0)[:].rearrange("p (t d) -> p t d", d=D),
                                    ROW0[:, 2:3, :].to_broadcast([P, 2, D]), ALU.mult).then_inc(dense_done, 1)
                elif what == "proj1":
                    wait(dve, hold_pool, at["hold"].at())
                    wait(dve, res_m_pool, at["gated_m"].at(2))
                    wait(dve, close_pool, at["close"].at(3))
                    for tp in range(2):
                        v.tensor_tensor(TMP[:, 2 * tp:2 * tp + 2, :], bank(tp)[:].rearrange("p (t d) -> p t d", d=D),
                                        RH[:, 2 * tp:2 * tp + 2, :], ALU.add).then_inc(dense_done, 1)
                elif what in ("sums0", "sums1"):
                    wait(dve, compact_dma, at["sums"].at(80, 80))
                    wait(dve, recip_dma, at["sums"].at(16))
                    v.reciprocal(RR[:], RS[:]).then_inc(recip_dve, 1)
                elif what == "keep0":
                    wait(dve, res_m_pool, at["gated_m"].at(2))
                    wait(dve, x_dma, at["x_in"].at(16))
                    v.tensor_copy(XR[:], XIN[:]).then_inc(keep_dve, 1)

            run_passes(dve, work, passed["dve"])

        @block.tensor
        def _(pe):
            t_ = nc.tensor
            pe.wait_ge(first_load, 16 * N_FIRST_LOAD)
            pe.wait_ge(set_dve, SILU_READY)
            for c in range(3):
                for k in range(KT):
                    ins = t_.matmul(SC[c][0:B, :], CS[:, k, :], WADA[:, k, c * T:c * T + T],
                                    start=k == 0, stop=k == KT - 1)
                ins.then_inc(set_pe, 1)
            for k in range(KT):
                ins = t_.matmul(OP[0:B, :], CT[:, k, :], WGB[:, k, :], start=k == 0, stop=k == KT - 1)
            ins.then_inc(set_pe, 1)
            pe.wait_ge(consts, N_CONSTS)
            pe.wait_ge(set_dve, ROWS_READY)
            for n, row in enumerate(BY_FEATURE):
                for ft in range(KT):
                    c = (n * KT + ft) * B
                    ins = t_.transpose(SX[0][:, c:c + B], ROWS[:, row, ft * P:ft * P + P], ID32[0:B, 0:B])
            ins.then_inc(set_pe, 1)
            pe.wait_ge(set_dve, FM_READY)
            pe.wait_ge(other_load, 16 * N_LOAD)
            marks = {}

            def pv(at, attend, s):
                g, kt = s // TT, s % TT
                lo = P * kt if attend == 0 else 0
                wait(pe, exp_done, at["head"].at())
                if kt == 0:
                    wait(pe, out_done, at["group"].at())
                for j in range(4):
                    h = 4 * g + j
                    ins = t_.matmul(OP[32 * j:32 * j + 32, lo:T], V[attend][:, kt, h * VW:h * VW + 32],
                                    E[:, (at["step"].index() - 1) % 2, j, lo:T],
                                    start=kt == 0, stop=kt == TT - 1)
                ins.then_inc(pv_done, 1)

            def score_t(at, attend, s, j):
                g, kt = s // TT, s % TT
                h = 4 * g + j
                lo = P * kt if attend == 0 else 0
                u = 4 * s + j
                wait(pe, exp_done, at["head"].at(1, j if u == 0 else j - 2))
                ins = t_.matmul(SC[u % 3][:, lo:T], KS[attend][0:ALL_ROWS, h, kt * P:kt * P + P],
                                QS[attend][0:ALL_ROWS, h, lo:T], start=True, stop=attend == 1)
                if attend == 0:
                    ins = t_.matmul(SC[u % 3][:, lo:lo + P], ID16[:], CAUSAL_T[:], start=False, stop=True)
                ins.then_inc(head_full, 1)

            def score(at, k, layer, h, qt):
                bank = SX[(at["scan"].index() + k) % 2]
                wait(pe, scan_done, at["scan"].at(1, k - 1))
                w = (qt + 1) * P if layer == 0 else T
                ins = t_.matmul(bank[:, 0:w], QS[layer][0:CUT_ROWS, h, qt * P:qt * P + P],
                                KS[layer][0:CUT_ROWS, h, 0:w], start=True, stop=layer == 1)
                if layer == 0:
                    ins = t_.matmul(bank[:, qt * P:w], ID16[:], CAUSAL[:], start=False, stop=True)
                ins.then_inc(scan_full, 1)

            def work(at, kind, what, b):
                if kind == "step":
                    s, attend, layer, heads = what
                    if s == 0 and attend is not None:
                        wait(pe, max_dma[attend], at[f"max{attend}"].at(16))
                        wait(pe, dense_done, at["dense"].at())
                    if heads and heads[0] == 0:
                        wait(pe, stack_dma[layer], at[f"stack{layer}"].at(192))
                    if attend is not None:
                        for j in range(3):
                            score_t(at, attend, s, j)
                    if heads:
                        score(at, 0, layer, heads[0], 0)
                        score(at, 1, layer, heads[0], 1)
                    if attend is not None:
                        if s > 0:
                            pv(at, attend, s - 1)
                        score_t(at, attend, s, 3)
                    if heads:
                        score(at, 2, layer, heads[0], 2)
                        score(at, 3, layer, heads[0], 3)
                    for n, h in enumerate(heads[1:]):
                        for qt in range(TT):
                            score(at, TT * (n + 1) + qt, layer, h, qt)
                    return
                if kind == "last":
                    pv(at, what, STEPS - 1)
                    return
                c = at["dense"]

                def bank(k):
                    wait(pe, dense_done, c.at(1, k - 1))
                    return DN[(c.index() + k) % 2]

                def by_token(k, rows, weights, tiles, depth):
                    psum = bank(k)
                    for n, t in enumerate(tiles):
                        for kt in range(depth):
                            ins = t_.matmul(psum[:, n * D:n * D + D], rows[:, kt, t * P:t * P + P],
                                            weights(kt), start=kt == 0, stop=kt == depth - 1)
                    ins.then_inc(dense_full, 1)

                if what in ("turn_a", "turn_m", "turn_1"):
                    wait(pe, norm_pool, at["norm"].at(6))
                    for ft in range(KT):
                        psum = bank(ft)
                        for t in range(TT):
                            ins = t_.transpose(psum[:, t * P:t * P + P], XN[:, t, ft * P:ft * P + P], ID32[:])
                        ins.then_inc(dense_full, 1)
                    marks["xt"] = c.at(1, 2)
                elif what in ("q0", "k0", "q1", "k1"):
                    side, n = "qk".index(what[0]), int(what[1])
                    wait(pe, dense_done, marks["xt"])
                    for t in range(2):
                        psum = bank(t)
                        for kt in range(KT):
                            lo = (2 * side + t) * P
                            ins = t_.matmul(psum[:], WQKV[n][:, kt, lo:lo + P], XT[:, kt, :],
                                            start=kt == 0, stop=kt == KT - 1)
                        ins.then_inc(dense_full, 1)
                elif what in ("v0", "v1"):
                    n = int(what[-1])
                    wait(pe, dense_done, marks["xt"])
                    for tp in range(2):
                        by_token(tp, XT, lambda kt: WQKV[n][:, kt, 2 * D:3 * D], (2 * tp, 2 * tp + 1), KT)
                elif what in ("proj0", "proj1"):
                    n = int(what[-1])
                    wait(pe, scaled_pool, at["sums"].at())
                    for tp in range(2):
                        by_token(tp, OC, lambda kt: WP[n][:, kt, :], (2 * tp, 2 * tp + 1), KT)
                elif what in ("up_a", "up_b"):
                    wait(pe, dense_done, marks["xt"])
                    for k in range(4):
                        ht = k + 4 * (what == "up_b")
                        psum = bank(k)
                        for kt in range(KT):
                            ins = t_.matmul(psum[:], W1[:, kt, ht * P:ht * P + P], XT[:, kt, :],
                                            start=kt == 0, stop=kt == KT - 1)
                        ins.then_inc(dense_full, 1)
                    marks["hid"] = c.at(1, 4)
                elif what in ("down_a", "down_b"):
                    tp = "ab".index(what[-1])
                    wait(pe, dense_done, marks["hid"])
                    by_token(0, HID, lambda ht: W2[:, ht, :], (2 * tp, 2 * tp + 1), FT)
                elif what in ("max0", "max1"):
                    psum = bank(0).bitcast(BF16)
                    wait(pe, max_pool, at["maxima"].at(4, 4), apart=True)
                    for qt in range(TT):
                        ins = t_.transpose(psum[0:3 * H, qt * P:qt * P + P],
                                           NMP[:, qt, :, :].rearrange("p a h -> p (a h)"), ID16[:])
                    ins.then_inc(dense_full, 1)

            run_passes(pe, work, passed["pe"])


SILU_READY, ROWS_READY, FM_READY = 3, 20, 21
N_FIRST_LOAD, N_LOAD = 16, 8
N_CONSTS = 13

_SHAPE = (B, T, D)


def kernel(**inputs):
    import concourse.bacc as bacc
    from concourse.bass_utils import run_bass_kernel_spmd

    a = {k: np.asarray(v) for k, v in inputs.items()}

    def qk_order(w):
        return w.reshape(-1, H // 2, 2, HD).transpose(0, 2, 3, 1).reshape(-1, D)

    def out_order(w):
        return w.reshape(GROUPS, 2, 2, HD, D).transpose(1, 2, 3, 0, 4).reshape(D, D)

    w0 = a["L0_cond_Wqkv"]
    w1 = a["L1_cond_Wqkv"].reshape(H, HD, 3, D).transpose(2, 3, 0, 1).reshape(3, D, D)
    bq1 = a["L1_cond_bqkv"].reshape(H, HD, 3).transpose(2, 0, 1).reshape(3, D)
    arrays = {
        "x": a["x"],
        "cond_t": a["cond_1024"].T,
        "wqkv0": np.concatenate([qk_order(w0[:, 0:D]), qk_order(w0[:, D:2 * D]), w0[:, 2 * D:]], axis=1),
        "wproj0": out_order(a["L0_cond_Wproj"]),
        "w1": a["L0_cond_W1"],
        "w2": a["L0_cond_W2"],
        "wada": a["L0_cond_Wada"],
        "wqkv1": np.concatenate([qk_order(w1[0]), qk_order(w1[1]), w1[2]], axis=1),
        "wp1": out_order(a["L1_cond_Wp"].T),
        "wgb1": np.concatenate([a["L1_cond_Wg"].T, a["L1_cond_Wb"].T], axis=1),
        "b1": a["L0_cond_b1"],
        "b_qk1": np.concatenate([qk_order(bq1[0:1])[0], qk_order(bq1[1:2])[0]]),
        "bv1": bq1[2],
        "bp1": a["L1_cond_bp"],
    }
    for name in ("L0_cond_bada", "L0_cond_bproj", "L0_cond_b2", "L0_cond_g1", "L0_cond_be1",
                 "L0_cond_g2", "L0_cond_be2", "L1_cond_ln_g", "L1_cond_ln_b", "L1_cond_bg", "L1_cond_bb"):
        arrays[name] = a[name]
    arrays = {f"in_{k}": np.ascontiguousarray(v) for k, v in arrays.items()}
    nc = bacc.Bacc("TRN2", target_bir_lowering=False, num_devices=1, dynamic_dma_scratch_size=1024)
    args = {k: nc.dram_tensor(k, v.shape, mybir.dt.from_np(v.dtype), kind="ExternalInput").ap()
            for k, v in arrays.items()}
    names = list(args)
    out = nc.dram_tensor("out", _SHAPE, F32, kind="ExternalOutput").ap()
    two_layers(nc, *(args[k] for k in names[:14]), [args[k] for k in names[14:]], out)
    r = run_bass_kernel_spmd(nc, [arrays], core_ids=[0])
    return r.results[0]["out"]
```

```python
from contextlib import ExitStack

import concourse.bass as bass
import numpy as np
from concourse import mybir

F32 = mybir.dt.float32
BF16 = mybir.dt.bfloat16
ALU = mybir.AluOpType
ACT = mybir.ActivationFunctionType
AX = mybir.AxisListType

P = 128
B, T, D = 8, 512, 256
H = 16
HD = D // H
F = 4 * D
EPS = 1e-5
TT = T // P
KT = D // P
FT = F // P
GROUPS = H // 4
CUTS = 6
CUT_ROWS = CUTS * HD
ALL_ROWS = CUT_ROWS + 3
Q_PARTS = (0, 0, 0, 1, 1, 2)
K_PARTS = (0, 1, 2, 0, 1, 0)
VW = HD + 1
VROW = H * VW + 16
STEPS = GROUPS * TT
MASKED = -3.0e38
GATE_A, GATE_A_BIAS, GATE_M, GATE_M_BIAS, NORM1, SHIFT1, NORM_A, SHIFT_A, NORM_M, SHIFT_M = range(10)
BY_FEATURE = (NORM_A, SHIFT_A, NORM_M, SHIFT_M, NORM1, SHIFT1)

SLOT_X = {0: ("recip0",), 1: ("stackk0", "v0"), 2: ("hold1",), 3: ("scale0",), 4: ("proj0",),
          5: ("norm_m", "turn_m"), 6: ("up_a",), 8: ("up_b",), 9: ("down_a",), 11: ("down_b", "keep0"),
          12: ("norm_1", "turn_1"), 14: ("q1",), 15: ("max0",)}
AFTER_X = ("pack1", "stackq1", "k1")
SLOT_Y = {0: ("stat_a", "recip1"), 1: ("stackk1", "v1", "norm_a"), 2: ("turn_a",), 3: ("scale1",),
          4: ("proj1",), 6: ("norm_o", "close1"), 9: ("q0",), 15: ("max1",)}
AFTER_Y = ("pack0", "stackq0", "k0")
BEHIND = {"recip0": 1, "hold1": 2, "scale0": 1, "proj0": 1, "norm_m": 1, "turn_m": 1, "up_a": 1,
          "up_b": 1, "down_a": 1, "down_b": 1, "keep0": 0, "norm_1": 1, "turn_1": 1, "q1": 1, "k1": 1,
          "v1": 1, "stackq1": 1, "stackk1": 1, "max0": 0, "pack1": 2, "recip1": 2, "scale1": 2,
          "proj1": 2, "norm_o": 2, "close1": 2, "stat_a": -1, "norm_a": -1, "turn_a": -1, "q0": -1,
          "k0": -1, "stackq0": -1, "stackk0": 0, "v0": 0, "pack0": 0, "max1": 1}
SCAN_X = [()] * 3 + [(0,), (1, 2), (3,), (4,), (5, 6), (7,), (8, 9), (10,), (11, 12), (13,), (14, 15)] + [()] * 2
SCAN_Y = [()] * 3 + [(0,), (1, 2), (3,), (4, 5), (6,), (7, 8), (9,), (10, 11), (12,), (13,), (14,), (15,), ()]
FIRST = ("stat_a", "norm_a", "turn_a", "q0", "stackq0", "k0")
ADDS = {"proj0": {"dense": 2, "res": 2}, "proj1": {"dense": 2}, "down_a": {"dense": 1, "res": 1},
        "down_b": {"dense": 1, "res": 1}, "up_a": {"dense": 4}, "up_b": {"dense": 4},
        "max0": {"dense": 1, "maxima": 1, "max0": 1}, "max1": {"dense": 1, "maxima": 1, "max1": 1},
        "hold1": {"hold": 1}, "recip0": {"sums": 1, "rows0": 1, "bias": 1},
        "recip1": {"sums": 1, "rows1": 1}, "pack0": {"pack": 1}, "pack1": {"pack": 1},
        "scale0": {"scale": 1}, "scale1": {"scale": 1},
        "keep0": {"keep": 1, "x_in": 1}, "close1": {"close": 1}, "stat_a": {},
        "stackq0": {}, "stackq1": {}, "stackk0": {"stack0": 1}, "stackk1": {"stack1": 1}}
for _n in ("turn_m", "turn_1", "turn_a", "v0", "v1"):
    ADDS[_n] = {"dense": 2}
for _n in ("q0", "k0", "q1", "k1"):
    ADDS[_n] = {"dense": 2, "cut": 1}
for _n in ("norm_m", "norm_1", "norm_a", "norm_o"):
    ADDS[_n] = {"norm": 1}
ADDS["norm_m"]["bias"] = 1
COUNTS = ("dense", "res", "bias", "maxima", "max0", "max1", "hold", "pack", "sums", "scale", "rows0",
          "rows1", "keep", "x_in", "close", "stack0", "stack1", "cut", "norm", "head", "step", "group",
          "scan")


class Loop:

    def __init__(self, eng, i, passed):
        self.eng, self.i, self.passed, self.registers = eng, i, passed, {}

    def apart(self):
        self.eng.sem_inc(self.passed, 1)

    def value(self, per, fixed):
        if per not in self.registers:
            pair = self.eng.alloc_register(f"grown_{per}"), self.eng.alloc_register(f"value_{per}")
            self.registers[per] = pair
            self.apart()
            self.eng.reg_mul(pair[0], self.i, per)
        grown, value = self.registers[per]
        if not fixed:
            return grown
        self.eng.reg_add(value, grown, fixed)
        return value


class Count:

    def __init__(self):
        self.n, self.start, self.loop, self.per = 0, 0, None, 0

    def enter(self, loop, first, per):
        self.start, self.n, self.loop, self.first, self.per = self.n, 0, loop, first, per

    def leave(self, passes):
        assert self.n == self.per, (self.n, self.per)
        self.n, self.loop = self.start + passes * self.per, None

    def at(self, times=1, add=0):
        if self.loop is None:
            return self.n * times + add
        fixed = (self.start - self.first * self.per + self.n) * times + add
        return self.loop, self.per * times, fixed

    def index(self):
        return self.n if self.loop is None else self.start + self.n


def per_pass():
    per = dict.fromkeys(COUNTS, 0)
    for slot in (*SLOT_X.values(), AFTER_X, *SLOT_Y.values(), AFTER_Y):
        for chunk in slot:
            for name, n in ADDS[chunk].items():
                per[name] += n
    per.update(head=2 * 4 * STEPS, step=2 * STEPS, group=2 * GROUPS, scan=2 * H * TT)
    return per


PER = per_pass()
FIRST_FULL, LAST_FULL = 3, B - 2


def wait(eng, sem, value, apart=False):
    if isinstance(value, int):
        if value > 0:
            eng.wait_ge(sem, value)
        return
    loop, per, fixed = value
    assert FIRST_FULL * per + fixed > 0, (per, fixed)
    eng.wait_ge(sem, loop.value(per, fixed))
    if apart:
        loop.apart()


def run_passes(eng, work, passed):
    at = {name: Count() for name in COUNTS}
    at["x_in"].n = 1
    for chunk in FIRST:
        do_chunk(at, work, chunk, 0)
    for i in range(FIRST_FULL):
        one_pass(at, work, i, i)
    with eng.Fori(FIRST_FULL, LAST_FULL + 1) as i:
        loop = Loop(eng, i, passed)
        for name in COUNTS:
            at[name].enter(loop, FIRST_FULL, PER[name])
        one_pass(at, work, i, None)
    for name in COUNTS:
        at[name].leave(LAST_FULL + 1 - FIRST_FULL)
    for i in range(LAST_FULL + 1, B + 2):
        one_pass(at, work, i, i)
    return at


def do_chunk(at, work, chunk, b):
    work(at, "chunk", chunk, b)
    for name, n in ADDS[chunk].items():
        at[name].n += n


def one_pass(at, work, i, number):

    def live(behind):
        return number is None or 0 <= number - behind < B

    for slot, after, attend, scan, heads in (
        (SLOT_X, AFTER_X, 1, 0, SCAN_X),
        (SLOT_Y, AFTER_Y, 0, 1, SCAN_Y),
    ):
        attending = live(2 if attend else 0)
        scanning = live(1 if scan else 0)
        for s in range(STEPS):
            work(at, "step", (s, attend if attending else None, scan, heads[s] if scanning else ()), i)
            if attending:
                at["head"].n += 4
                at["step"].n += 1
                at["group"].n += s > 0 and s % TT == 0
            at["scan"].n += TT * len(heads[s]) if scanning else 0
            for chunk in slot.get(s, ()):
                if live(BEHIND[chunk]):
                    do_chunk(at, work, chunk, i - BEHIND[chunk])
        if attending:
            work(at, "last", attend, i)
            at["group"].n += 1
        for chunk in after:
            if live(BEHIND[chunk]):
                do_chunk(at, work, chunk, i - BEHIND[chunk])


def two_layers(nc, x, cond_t, wqkv0, wproj0, w1, w2, wada, wqkv1, wp1, wgb1, b1, b_qk1, bv1, bp1,
               vectors, out):
    ctx = ExitStack()
    with ctx:
        def sb(name, shape, dt=F32):
            return ctx.enter_context(nc.sbuf_tensor(name, shape, dt))

        def pb(name, shape, dt=F32):
            return ctx.enter_context(nc.psum_tensor(name, shape, dt))

        def sem(name):
            return ctx.enter_context(nc.semaphore(name))

        WQKV = [sb("WQKV0", [P, KT, 3 * D]), sb("WQKV1", [P, KT, 3 * D])]
        WP = [sb("WP0", [P, KT, D]), sb("WP1", [P, KT, D])]
        W1 = sb("W1", [P, KT, F])
        W2 = sb("W2", [P, FT, D])
        B1 = sb("B1", [P, FT])
        BQK1 = sb("BQK1", [P, 4])
        BV1 = sb("BV1", [P, D])
        BP1 = sb("BP1", [P, D])
        QS = [sb("QS0", [P, H, T], BF16), sb("QS1", [P, H, T], BF16)]
        KS = [sb("KS0", [P, H, T], BF16), sb("KS1", [P, H, T], BF16)]
        V = [sb("V0", [P, TT, VROW]), sb("V1", [P, TT, VROW])]
        E = sb("E", [P, 2, 4, T])
        HID = sb("HID", [P, FT, T])
        OE = sb("OE", [P, GROUPS, T])
        OC = sb("OC", [P, KT, T])
        RB = sb("RB", [P, KT, T])
        RS = sb("RS", [P, T // 8])
        RR = sb("RR", [P, T // 8])
        XIN = sb("XIN", [P, TT, D])
        XR = sb("XR", [P, TT, D])
        R1 = sb("R1", [P, TT, D])
        RH = sb("RH", [P, TT, D])
        TMP = sb("TMP", [P, TT, D])
        XN = sb("XN", [P, TT, D])
        OUT = sb("OUT", [P, TT, D])
        XT = sb("XT", [P, KT, T])
        X32 = sb("X32", [P, 2, T])
        PART = sb("PART", [P, 2, 3, 2, T], BF16)
        ROW0 = sb("ROW0", [P, 4, D])
        ROW1 = sb("ROW1", [P, 2, D])
        NT = sb("NT", [3 * H, T], BF16)
        MX = sb("MX", [P, TT, H])
        MR = sb("MR", [P, TT, H])
        NMP = sb("NMP", [P, TT, 3, H], BF16)
        STAT = sb("STAT", [P, TT, 6])
        MV = sb("MV", [P, TT, 2])
        VE = sb("VE", [P, TT])
        RSTD = sb("RSTD", [P, TT])
        HALF = sb("HALF", [P, TT])
        FM = sb("FM", [P, len(BY_FEATURE) * KT, B])
        ID32 = sb("ID32", [P, P])
        ID16 = sb("ID16", [P, P], BF16)
        CAUSAL = sb("CAUSAL", [P, P], BF16)
        CAUSAL_T = sb("CAUSAL_T", [P, P], BF16)
        CT = sb("CT", [P, KT, B])
        CE = sb("CE", [P, KT, B])
        CS = sb("CS", [P, KT, B])
        WADA = HID[:, 0:6, :].rearrange("p a b -> p (a b)").rearrange("p (k n) -> p k n", k=KT)
        WGB = E[:, 0, 0:2, :]
        MODS = OE[0:B, 0:3, :].rearrange("p a b -> p (a b)")
        GB = OE[0:B, 3, :]
        ROWS = QS[0].bitcast(F32)[0:B, 0:10, :]
        VEC = QS[1].bitcast(F32)[0:B, :, :].rearrange("p a b -> p (a b)")

        SC = [pb(f"SC{i}", [P, T]) for i in range(3)]
        DN = [pb(f"DN{i}", [P, T]) for i in range(2)]
        SX = [pb(f"SX{i}", [P, T]) for i in range(2)]
        OP = pb("OP", [P, T])

        sums_dram = nc.dram_tensor("recip_sums", (4, GROUPS, T), F32, kind="Internal").ap()
        rows_dram = nc.dram_tensor("row_vectors", (B, 6, D), F32, kind="Internal").ap()

        first_load = sem("first_load")
        other_load = sem("other_load")
        consts = sem("consts")
        set_act = sem("set_act")
        set_dve = sem("set_dve")
        set_pe = sem("set_pe")
        rows_out = sem("rows_out")
        x_dma = sem("x_dma")
        dense_full = sem("dense_full")
        dense_done = sem("dense_done")
        head_full = sem("head_full")
        exp_done = sem("exp_done")
        scan_full = sem("scan_full")
        scan_done = sem("scan_done")
        pv_done = sem("pv_done")
        out_done = sem("out_done")
        stat_dve = sem("stat_dve")
        rstd_pool = sem("rstd_pool")
        norm_dve = sem("norm_dve")
        high_dve = sem("high_dve")
        cut_pool = sem("cut_pool")
        max_pool = sem("max_pool")
        max_dma = [sem("max_dma0"), sem("max_dma1")]
        stack_dma = [sem("stack_dma0"), sem("stack_dma1")]
        compact_dma = sem("compact_dma")
        recip_dve = sem("recip_dve")
        recip_dma = sem("recip_dma")
        spread_dma = sem("spread_dma")
        scaled_dve = sem("scaled_dve")
        row0_dma = sem("row0_dma")
        row1_dma = sem("row1_dma")
        bias_pool = sem("bias_pool")
        res_dve = sem("res_dve")
        hold_pool = sem("hold_pool")
        keep_dve = sem("keep_dve")
        close_pool = sem("close_pool")
        store_dma = sem("store_dma")

        passed = {name: sem(f"passed_{name}") for name in ("sp", "pool", "act", "dve", "pe")}

        block = ctx.enter_context(nc.Block())

        @block.sync
        def _(sp):
            sp.dma_start(CT[:], cond_t.rearrange("(k p) b -> p k b", p=P)).then_inc(first_load, 16)
            sp.dma_start(WADA, wada.rearrange("(k p) n -> p k n", p=P)).then_inc(first_load, 16)
            sp.dma_start(WGB, wgb1.rearrange("(k p) n -> p k n", p=P)).then_inc(first_load, 16)
            at_col = 0
            for v in vectors:
                n = v.shape[0]
                sp.dma_start(VEC[:, at_col:at_col + n],
                             v.unsqueeze(0).to_broadcast([B, n])).then_inc(first_load, 16)
                at_col += n
            sp.dma_start(WQKV[0][:], wqkv0.rearrange("(k p) n -> p k n", p=P)).then_inc(first_load, 16)
            sp.dma_start(WP[0][:], wproj0.rearrange("(k p) n -> p k n", p=P)).then_inc(first_load, 16)
            sp.dma_start(XIN[:], x[0].rearrange("(t p) d -> p t d", p=P)).then_inc(x_dma, 16)
            sp.dma_start(W1[:], w1.rearrange("(k p) n -> p k n", p=P)).then_inc(other_load, 16)
            sp.dma_start(W2[:], w2.rearrange("(k p) n -> p k n", p=P)).then_inc(other_load, 16)
            sp.dma_start(WQKV[1][:], wqkv1.rearrange("(k p) n -> p k n", p=P)).then_inc(other_load, 16)
            sp.dma_start(WP[1][:], wp1.rearrange("(k p) n -> p k n", p=P)).then_inc(other_load, 16)
            with nc.allow_non_contiguous_dma(reason="small bias vectors by feature"):
                sp.dma_start(B1[:], b1.rearrange("(k p) -> p k", p=P)).then_inc(other_load, 16)
                sp.dma_start(BQK1[:], b_qk1.rearrange("(k p) -> p k", p=P)).then_inc(other_load, 16)
            sp.dma_start(BV1[:], bv1.unsqueeze(0).to_broadcast([P, D])).then_inc(other_load, 16)
            sp.dma_start(BP1[:], bp1.unsqueeze(0).to_broadcast([P, D])).then_inc(other_load, 16)
            sp.wait_ge(set_dve, ROWS_READY)
            sp.dma_start(rows_dram, ROWS[:, 0:6, :]).then_inc(rows_out, 16)
            sp.wait_ge(rows_out, 16)

            def work(at, kind, what, b):
                if kind != "chunk":
                    return
                if what in ("pack0", "pack1"):
                    wait(sp, out_done, at["group"].at(), apart=True)
                    wait(sp, dense_full, at["dense"].at(), apart=True)
                    wait(sp, recip_dve, at["sums"].at(), apart=True)
                    sp.dma_start(RS[:], OE[HD:P:32, :, :]).then_inc(compact_dma, 16)
                    for j in range(4):
                        sp.dma_start(OC[64 * (j % 2):64 * (j % 2) + 64, j // 2, :],
                                     OE[32 * j:32 * j + HD, :, :]).then_inc(compact_dma, 16)
                elif what in ("recip0", "recip1"):
                    wait(sp, recip_dve, at["sums"].at(1, 1), apart=True)
                    wait(sp, spread_dma, at["sums"].at(64), apart=True)
                    sp.dma_start(sums_dram.rearrange("j g (c n) -> (j g c) n", c=8), RR[:])\
                        .then_inc(recip_dma, 16)
                    wait(sp, recip_dma, at["sums"].at(16, 16), apart=True)
                    wait(sp, scaled_dve, at["sums"].at(), apart=True)
                    for j in range(4):
                        sp.dma_start(RB[64 * (j % 2):64 * (j % 2) + 64, j // 2, :],
                                     sums_dram[j].unsqueeze(0).to_broadcast([HD, GROUPS, T]))\
                            .then_inc(spread_dma, 16)
                    if what == "recip0":
                        wait(sp, bias_pool, at["bias"].at(), apart=True)
                        wait(sp, res_dve, at["res"].at(), apart=True)
                        sp.dma_start(ROW0[:], rows_dram[bass.ds(b, 1), 0:4, :].to_broadcast([P, 4, D]))\
                            .then_inc(row0_dma, 16)
                    else:
                        wait(sp, close_pool, at["close"].at(3), apart=True)
                        sp.dma_start(ROW1[:], rows_dram[bass.ds(b, 1), 4:6, :].to_broadcast([P, 2, D]))\
                            .then_inc(row1_dma, 16)
                elif what == "keep0":
                    wait(sp, keep_dve, at["keep"].at(1, 1), apart=True)
                    if not isinstance(b, int) or b + 1 < B:
                        sp.dma_start(XIN[:], x[bass.ds(b + 1, 1)].rearrange("a (t p) d -> p (a t) d", p=P))\
                            .then_inc(x_dma, 16)
                elif what == "close1":
                    wait(sp, close_pool, at["close"].at(3, 3), apart=True)
                    sp.dma_start(out[bass.ds(b, 1)].rearrange("a (t p) d -> p (a t) d", p=P), OUT[:])\
                        .then_inc(store_dma, 16)
                elif what in ("stackq0", "stackq1", "stackk0", "stackk1"):
                    n, side = int(what[-1]), "qk".index(what[5])
                    wait(sp, high_dve, at["cut"].at(), apart=True)
                    wait(sp, cut_pool, at["cut"].at(3), apart=True)
                    if side == 0:
                        wait(sp, pv_done, at["step"].at(), apart=True)
                    for r in range(CUTS):
                        sp.dma_start((QS, KS)[side][n][HD * r:HD * r + HD, :, :],
                                     PART[:, side, (Q_PARTS, K_PARTS)[side][r], :, :])\
                            .then_inc(stack_dma[n], 16)

            run_passes(sp, work, passed["sp"])
            sp.wait_ge(store_dma, 16 * B)

        @block.gpsimd
        def _(pool):
            g = nc.gpsimd
            g.memset(ID32[:], 0.0).then_inc(consts, 1)
            g.memset(ID16[:], 0.0).then_inc(consts, 1)
            g.memset(CAUSAL[:], 0.0).then_inc(consts, 1)
            g.memset(CAUSAL_T[:], 0.0).then_inc(consts, 1)
            pool.wait_ge(consts, 4)
            for m in (ID32, ID16):
                g.affine_select(out=m[:], in_=m[:], compare_op=ALU.not_equal, fill=1.0, base=0,
                                pattern=[[-1, P]], channel_multiplier=1).then_inc(consts, 1)
            g.affine_select(out=CAUSAL[:], in_=CAUSAL[:], compare_op=ALU.is_ge, fill=MASKED, base=0,
                            pattern=[[-1, P]], channel_multiplier=1).then_inc(consts, 1)
            g.affine_select(out=CAUSAL_T[:], in_=CAUSAL_T[:], compare_op=ALU.is_ge, fill=MASKED, base=0,
                            pattern=[[1, P]], channel_multiplier=-1).then_inc(consts, 1)
            g.memset(HALF[:], -0.5).then_inc(consts, 1)
            g.memset(V[0][:], 1.0).then_inc(consts, 1)
            g.memset(V[1][:], float(D) ** 0.5).then_inc(consts, 1)
            pool.wait_ge(consts, N_CONSTS - 2)
            g.memset(KS[0][CUT_ROWS:ALL_ROWS, :, :], 1.0).then_inc(consts, 1)
            pool.wait_ge(consts, N_CONSTS - 1)
            g.memset(KS[1][CUT_ROWS:ALL_ROWS, :, :], 1.0).then_inc(consts, 1)
            pool.wait_ge(consts, N_CONSTS)

            def work(at, kind, what, b):
                if kind != "chunk":
                    return
                if what in ("stat_a", "proj0", "down_b", "proj1"):
                    wait(pool, stat_dve, at["norm"].at(9, 9), apart=True)
                    g.tensor_tensor(RSTD[:], VE[:], HALF[:], ALU.pow).then_inc(rstd_pool, 1)
                elif what == "norm_m":
                    wait(pool, norm_dve, at["norm"].at(4, 4), apart=True)
                    g.tensor_tensor(XR[:], XR[:], ROW0[:, 3:4, :].to_broadcast([P, TT, D]), ALU.add)\
                        .then_inc(bias_pool, 1)
                elif what in ("q0", "k0", "q1", "k1"):
                    side = "qk".index(what[0])
                    part = PART[:, side, :, :, :]
                    c = at["cut"]
                    wait(pool, high_dve, c.at(1, 1), apart=True)
                    wait(pool, stack_dma[0], at["stack0"].at(192), apart=True)
                    wait(pool, stack_dma[1], at["stack1"].at(192), apart=True)
                    g.tensor_tensor(X32[:], X32[:], part[:, 0], ALU.subtract).then_inc(cut_pool, 1)
                    wait(pool, cut_pool, c.at(3, 1), apart=True)
                    g.tensor_scalar(part[:, 1], X32[:], 1.0, 0.0, ALU.mult, ALU.add).then_inc(cut_pool, 1)
                    wait(pool, cut_pool, c.at(3, 2), apart=True)
                    g.tensor_tensor(part[:, 2], X32[:], part[:, 1], ALU.subtract).then_inc(cut_pool, 1)
                elif what in ("max0", "max1"):
                    m = at["maxima"]
                    wait(pool, scan_done, at["scan"].at(), apart=True)
                    wait(pool, dense_full, at["dense"].at(), apart=True)
                    g.tensor_scalar(NMP[:, :, 0, :], MX[:], 1.0, 0.0, ALU.mult, ALU.add).then_inc(max_pool, 1)
                    wait(pool, max_pool, m.at(4, 1), apart=True)
                    g.tensor_tensor(MR[:], MX[:], NMP[:, :, 0, :], ALU.subtract).then_inc(max_pool, 1)
                    wait(pool, max_pool, m.at(4, 2), apart=True)
                    g.tensor_scalar(NMP[:, :, 1, :], MR[:], 1.0, 0.0, ALU.mult, ALU.add).then_inc(max_pool, 1)
                    wait(pool, max_pool, m.at(4, 3), apart=True)
                    g.tensor_tensor(NMP[:, :, 2, :], MR[:], NMP[:, :, 1, :], ALU.subtract).then_inc(max_pool, 1)
                elif what == "recip0":
                    wait(pool, row0_dma, at["rows0"].at(16, 16), apart=True)
                    wait(pool, keep_dve, at["keep"].at(), apart=True)
                    g.tensor_tensor(XR[:], XR[:], ROW0[:, 1:2, :].to_broadcast([P, TT, D]), ALU.add)\
                        .then_inc(bias_pool, 1)
                elif what == "hold1":
                    wait(pool, res_dve, at["res"].at(), apart=True)
                    wait(pool, other_load, 16 * N_LOAD, apart=True)
                    wait(pool, dense_done, at["dense"].at(), apart=True)
                    g.tensor_tensor(RH[:], R1[:], BP1[:].unsqueeze(1).to_broadcast([P, TT, D]), ALU.add)\
                        .then_inc(hold_pool, 1)
                elif what == "close1":
                    c = at["close"]
                    wait(pool, norm_dve, at["norm"].at(4), apart=True)
                    wait(pool, row1_dma, at["rows1"].at(16), apart=True)
                    g.tensor_tensor(OUT[:], OUT[:], ROW1[:, 0:1, :].to_broadcast([P, TT, D]), ALU.mult)\
                        .then_inc(close_pool, 1)
                    g.tensor_tensor(TMP[:], TMP[:], ROW1[:, 1:2, :].to_broadcast([P, TT, D]), ALU.add)\
                        .then_inc(close_pool, 1)
                    wait(pool, close_pool, c.at(3, 2), apart=True)
                    g.tensor_tensor(OUT[:], OUT[:], TMP[:], ALU.add).then_inc(close_pool, 1)

            run_passes(pool, work, passed["pool"])

        @block.scalar
        def _(act):
            a = nc.scalar
            act.wait_ge(first_load, 16 * N_FIRST_LOAD)
            a.activation(CE[:], CT[:], ACT.Exp, scale=-1.0).then_inc(set_act, 1)
            act.wait_ge(other_load, 16 * N_LOAD)
            act.wait_ge(set_dve, FM_READY)

            def work(at, kind, what, b):
                if kind == "step":
                    s, attend, _, _ = what
                    if attend is None:
                        return
                    lo = P * (s % TT) if attend == 0 else 0
                    for j in range(4):
                        if j == 0:
                            wait(act, pv_done, at["step"].at(1, -1))
                        wait(act, head_full, at["head"].at(1, j + 1))
                        a.activation(E[:, at["step"].index() % 2, j, lo:T], SC[(4 * s + j) % 3][:, lo:T],
                                     ACT.Exp, scale=HD ** -0.5 if attend == 0 else 1.0)\
                            .then_inc(exp_done, 1)
                    return
                if kind != "chunk":
                    return
                c = at["dense"]

                def bank(k):
                    wait(act, dense_full, c.at(1, k + 1))
                    return DN[(c.index() + k) % 2]

                if what in ("turn_a", "turn_m", "turn_1"):
                    first = {"turn_a": 0, "turn_m": 2, "turn_1": 4}[what]
                    for ft in range(KT):
                        a.activation(XT[:, ft, :], bank(ft)[:], ACT.Identity,
                                     scale=FM[:, first * KT + ft, bass.ds(b, 1)],
                                     bias=FM[:, (first + 1) * KT + ft, bass.ds(b, 1)])\
                            .then_inc(dense_done, 1)
                elif what in ("q0", "k0", "q1", "k1"):
                    side = "qk".index(what[0])
                    wait(act, cut_pool, at["cut"].at(3))
                    wait(act, high_dve, at["cut"].at())
                    for t in range(2):
                        if what[1] == "0":
                            ins = a.activation(X32[:, t, :], bank(t)[:], ACT.Copy)
                        else:
                            ins = a.activation(X32[:, t, :], bank(t)[:], ACT.Identity,
                                               bias=BQK1[:, 2 * side + t:2 * side + t + 1])
                        ins.then_inc(dense_done, 1)
                elif what in ("up_a", "up_b"):
                    for k in range(4):
                        ht = k + 4 * (what == "up_b")
                        a.activation(HID[:, ht, :], bank(k)[:], ACT.Gelu, bias=B1[:, ht:ht + 1])\
                            .then_inc(dense_done, 1)
                elif what in ("max0", "max1"):
                    n = int(what[-1])
                    psum = bank(0)
                    wait(act, max_dma[0], at["max0"].at(16))
                    wait(act, max_dma[1], at["max1"].at(16))
                    a.activation(NT[:], psum.bitcast(BF16)[0:3 * H, 0:T], ACT.Copy).then_inc(dense_done, 1)
                    wait(act, dense_done, c.at(1, 1))
                    act.dma_start(QS[n][CUT_ROWS:ALL_ROWS, :, :], NT[:]).then_inc(max_dma[n], 16)

            run_passes(act, work, passed["act"])

        @block.vector
        def _(dve):
            v = nc.vector
            done = [0]

            def then(ins):
                done[0] += 1
                ins.then_inc(set_dve, 1)
                return done[0]

            dve.wait_ge(set_act, 1)
            n = then(v.tensor_scalar(CE[:], CE[:], 1.0, 1.0, ALU.mult, ALU.add))
            dve.wait_ge(set_dve, n)
            n = then(v.reciprocal(CE[:], CE[:]))
            dve.wait_ge(set_dve, n)
            n = then(v.tensor_tensor(CS[:], CT[:], CE[:], ALU.mult))
            assert n == SILU_READY
            dve.wait_ge(first_load, 16 * N_FIRST_LOAD)
            for c in range(3):
                dve.wait_ge(set_pe, c + 1)
                then(v.tensor_tensor(MODS[:, c * T:c * T + T], SC[c][0:B, :], VEC[:, c * T:c * T + T], ALU.add))
            dve.wait_ge(set_pe, 4)
            n = then(v.tensor_tensor(GB, OP[0:B, :], VEC[:, 6 * D + 8 * D:6 * D + 10 * D], ALU.add))
            dve.wait_ge(set_dve, n)

            def mod(k):
                return MODS[:, k * D:k * D + D]

            def vec(k):
                return VEC[:, (6 + k) * D:(7 + k) * D]

            (bproj, b2, g1, be1, g2, be2, ln_g, ln_b) = (vec(k) for k in range(8))
            (shift_a, scale_a, gate_a, shift_m, scale_m, gate_m) = (mod(k) for k in range(6))
            gamma, beta = GB[:, 0:D], GB[:, D:2 * D]
            then(v.tensor_copy(ROWS[:, GATE_A, :], gate_a))
            then(v.tensor_tensor(ROWS[:, GATE_A_BIAS, :], gate_a, bproj, ALU.mult))
            then(v.tensor_copy(ROWS[:, GATE_M, :], gate_m))
            then(v.tensor_tensor(ROWS[:, GATE_M_BIAS, :], gate_m, b2, ALU.mult))
            then(v.tensor_tensor(ROWS[:, NORM1, :], gamma, ln_g, ALU.mult))
            then(v.tensor_tensor(ROWS[:, SHIFT1, :], gamma, ln_b, ALU.mult))
            then(v.scalar_tensor_tensor(ROWS[:, NORM_A, :], scale_a, 1.0, g1, ALU.add, ALU.mult))
            then(v.scalar_tensor_tensor(ROWS[:, SHIFT_A, :], scale_a, 1.0, be1, ALU.add, ALU.mult))
            then(v.scalar_tensor_tensor(ROWS[:, NORM_M, :], scale_m, 1.0, g2, ALU.add, ALU.mult))
            n = then(v.scalar_tensor_tensor(ROWS[:, SHIFT_M, :], scale_m, 1.0, be2, ALU.add, ALU.mult))
            dve.wait_ge(set_dve, n)
            for row, plus in ((SHIFT1, beta), (SHIFT_A, shift_a), (SHIFT_M, shift_m)):
                n = then(v.tensor_tensor(ROWS[:, row, :], ROWS[:, row, :], plus, ALU.add))
            assert n == ROWS_READY
            dve.wait_ge(set_pe, 5)
            n = then(v.tensor_copy(FM[:], SX[0][:, 0:len(BY_FEATURE) * KT * B]
                                   .rearrange("p (k b) -> p k b", b=B)))
            assert n == FM_READY
            dve.wait_ge(set_dve, n)
            dve.wait_ge(consts, N_CONSTS)
            dve.wait_ge(other_load, 16 * N_LOAD)

            def scan(at, k, scan_head, qt):
                wait(dve, scan_full, at["scan"].at(1, k + 1))
                w = (qt + 1) * P if scan_head[0] == 0 else T
                v.reduce_max(MX[:, qt, scan_head[1]:scan_head[1] + 1],
                             SX[(at["scan"].index() + k) % 2][:, 0:w], AX.X, negate=True)\
                    .then_inc(scan_done, 1)

            def take_out(at, g):
                wait(dve, pv_done, at["step"].at())
                wait(dve, compact_dma, at["pack"].at(80))
                v.tensor_copy(OE[:, g, :], OP[:]).then_inc(out_done, 1)

            def stats(at, src):
                c = at["norm"]
                for t in range(TT):
                    v.bn_stats(STAT[:, t, :], src[:, t, :]).then_inc(stat_dve, 1)
                wait(dve, stat_dve, c.at(9, 4), apart=True)
                for t in range(TT):
                    v.bn_aggr(MV[:, t, :], STAT[:, t, :]).then_inc(stat_dve, 1)
                wait(dve, stat_dve, c.at(9, 8), apart=True)
                v.tensor_scalar(VE[:], MV[:, :, 1], 1.0, EPS, ALU.mult, ALU.add).then_inc(stat_dve, 1)

            def work(at, kind, what, b):
                if kind == "step":
                    s, attend, layer, heads = what
                    if heads and heads[0] == 0:
                        wait(dve, max_pool, at["maxima"].at(4))
                    out_now = attend is not None and s > 0 and s % TT == 0
                    if heads:
                        scan(at, 0, (layer, heads[0]), 0)
                        scan(at, 1, (layer, heads[0]), 1)
                    if out_now:
                        take_out(at, s // TT - 1)
                    if heads:
                        scan(at, 2, (layer, heads[0]), 2)
                        scan(at, 3, (layer, heads[0]), 3)
                    for n, h in enumerate(heads[1:]):
                        for qt in range(TT):
                            scan(at, TT * (n + 1) + qt, (layer, h), qt)
                    return
                if kind == "last":
                    take_out(at, GROUPS - 1)
                    return
                c = at["dense"]

                def bank(k):
                    wait(dve, dense_full, c.at(1, k + 1))
                    return DN[(c.index() + k) % 2]

                if what == "stat_a":
                    wait(dve, x_dma, at["x_in"].at(16))
                    stats(at, XIN)
                elif what in ("norm_a", "norm_m", "norm_1", "norm_o"):
                    src = {"norm_a": XIN, "norm_m": XR, "norm_1": R1, "norm_o": TMP}[what]
                    dst = OUT if what == "norm_o" else XN
                    wait(dve, rstd_pool, at["norm"].at(1, 1))
                    if what == "norm_o":
                        wait(dve, store_dma, at["close"].at(16))
                    else:
                        wait(dve, dense_full, c.at())
                    for t in range(TT):
                        v.tensor_scalar(dst[:, t, :], src[:, t, :], MV[:, t, 0:1], RSTD[:, t:t + 1],
                                        ALU.subtract, ALU.mult).then_inc(norm_dve, 1)
                elif what in ("q0", "k0", "q1", "k1"):
                    side = "qk".index(what[0])
                    wait(dve, dense_done, c.at(1, 2))
                    wait(dve, stack_dma[0], at["stack0"].at(192))
                    wait(dve, stack_dma[1], at["stack1"].at(192))
                    v.tensor_copy(PART[:, side, 0, :, :], X32[:]).then_inc(high_dve, 1)
                elif what in ("v0", "v1"):
                    n = int(what[-1])
                    for tp in range(2):
                        psum = bank(tp)[:].rearrange("p (t h d) -> p t h d", t=2, d=HD)
                        for t in range(2):
                            dst = V[n][:, 2 * tp + t, 0:H * VW].rearrange("p (h e) -> p h e", e=VW)[:, :, 0:HD]
                            if n == 0:
                                ins = v.tensor_copy(dst, psum[:, t])
                            else:
                                ins = v.tensor_tensor(dst, psum[:, t],
                                                      BV1[:].rearrange("p (h d) -> p h d", d=HD), ALU.add)
                        ins.then_inc(dense_done, 1)
                elif what in ("proj0", "down_a", "down_b"):
                    wait(dve, row0_dma, at["rows0"].at(16))
                    wait(dve, bias_pool, at["bias"].at())
                    if what == "proj0":
                        wait(dve, close_pool, at["close"].at(3))
                    if what == "down_a":
                        wait(dve, hold_pool, at["hold"].at())
                    gate, dst = (0, XR) if what == "proj0" else (2, R1)
                    pairs = (0, 1) if what == "proj0" else ("ab".index(what[-1]),)
                    for n, tp in enumerate(pairs):
                        two = slice(2 * tp, 2 * tp + 2)
                        v.tensor_tensor(TMP[:, two, :], bank(n)[:].rearrange("p (t d) -> p t d", d=D),
                                        ROW0[:, gate:gate + 1, :].to_broadcast([P, 2, D]), ALU.mult)\
                            .then_inc(dense_done, 1)
                        wait(dve, dense_done, c.at(1, n + 1))
                        v.tensor_tensor(dst[:, two, :], XR[:, two, :], TMP[:, two, :], ALU.add)\
                            .then_inc(res_dve, 1)
                    if what != "down_a":
                        wait(dve, res_dve, at["res"].at(1, len(pairs)))
                        stats(at, dst)
                elif what == "proj1":
                    wait(dve, hold_pool, at["hold"].at())
                    for tp in range(2):
                        v.tensor_tensor(TMP[:, 2 * tp:2 * tp + 2, :], bank(tp)[:].rearrange("p (t d) -> p t d", d=D),
                                        RH[:, 2 * tp:2 * tp + 2, :], ALU.add).then_inc(dense_done, 1)
                    wait(dve, dense_done, c.at(1, 2))
                    stats(at, TMP)
                elif what in ("recip0", "recip1"):
                    wait(dve, compact_dma, at["pack"].at(80))
                    wait(dve, recip_dma, at["sums"].at(16))
                    v.reciprocal(RR[:], RS[:]).then_inc(recip_dve, 1)
                elif what in ("scale0", "scale1"):
                    wait(dve, spread_dma, at["sums"].at(64))
                    v.tensor_tensor(OC[:], OC[:], RB[:], ALU.mult).then_inc(scaled_dve, 1)
                elif what == "keep0":
                    wait(dve, x_dma, at["x_in"].at(16))
                    v.tensor_copy(XR[:], XIN[:]).then_inc(keep_dve, 1)

            run_passes(dve, work, passed["dve"])

        @block.tensor
        def _(pe):
            t_ = nc.tensor
            pe.wait_ge(first_load, 16 * N_FIRST_LOAD)
            pe.wait_ge(set_dve, SILU_READY)
            for c in range(3):
                for k in range(KT):
                    ins = t_.matmul(SC[c][0:B, :], CS[:, k, :], WADA[:, k, c * T:c * T + T],
                                    start=k == 0, stop=k == KT - 1)
                ins.then_inc(set_pe, 1)
            for k in range(KT):
                ins = t_.matmul(OP[0:B, :], CT[:, k, :], WGB[:, k, :], start=k == 0, stop=k == KT - 1)
            ins.then_inc(set_pe, 1)
            pe.wait_ge(consts, N_CONSTS)
            pe.wait_ge(set_dve, ROWS_READY)
            for n, row in enumerate(BY_FEATURE):
                for ft in range(KT):
                    c = (n * KT + ft) * B
                    ins = t_.transpose(SX[0][:, c:c + B], ROWS[:, row, ft * P:ft * P + P], ID32[0:B, 0:B])
            ins.then_inc(set_pe, 1)
            pe.wait_ge(set_dve, FM_READY)
            pe.wait_ge(other_load, 16 * N_LOAD)
            marks = {}

            def pv(at, attend, s):
                g, kt = s // TT, s % TT
                lo = P * kt if attend == 0 else 0
                wait(pe, exp_done, at["head"].at())
                if s == 0:
                    wait(pe, dense_done, at["dense"].at())
                if kt == 0:
                    wait(pe, out_done, at["group"].at())
                for j in range(4):
                    h = 4 * g + j
                    ins = t_.matmul(OP[32 * j:32 * j + 32, lo:T], V[attend][:, kt, h * VW:h * VW + 32],
                                    E[:, (at["step"].index() - 1) % 2, j, lo:T],
                                    start=kt == 0, stop=kt == TT - 1)
                ins.then_inc(pv_done, 1)

            def score_t(at, attend, s, j):
                g, kt = s // TT, s % TT
                h = 4 * g + j
                lo = P * kt if attend == 0 else 0
                u = 4 * s + j
                wait(pe, exp_done, at["head"].at(1, j if u == 0 else j - 2))
                ins = t_.matmul(SC[u % 3][:, lo:T], KS[attend][0:ALL_ROWS, h, kt * P:kt * P + P],
                                QS[attend][0:ALL_ROWS, h, lo:T], start=True, stop=attend == 1)
                if attend == 0:
                    ins = t_.matmul(SC[u % 3][:, lo:lo + P], ID16[:], CAUSAL_T[:], start=False, stop=True)
                ins.then_inc(head_full, 1)

            def score(at, k, layer, h, qt):
                bank = SX[(at["scan"].index() + k) % 2]
                wait(pe, scan_done, at["scan"].at(1, k - 1))
                w = (qt + 1) * P if layer == 0 else T
                ins = t_.matmul(bank[:, 0:w], QS[layer][0:CUT_ROWS, h, qt * P:qt * P + P],
                                KS[layer][0:CUT_ROWS, h, 0:w], start=True, stop=layer == 1)
                if layer == 0:
                    ins = t_.matmul(bank[:, qt * P:w], ID16[:], CAUSAL[:], start=False, stop=True)
                ins.then_inc(scan_full, 1)

            def work(at, kind, what, b):
                if kind == "step":
                    s, attend, layer, heads = what
                    if s == 0 and attend is not None:
                        wait(pe, max_dma[attend], at[f"max{attend}"].at(16))
                    if heads and heads[0] == 0:
                        wait(pe, stack_dma[layer], at[f"stack{layer}"].at(192))
                    if attend is not None:
                        for j in range(3):
                            score_t(at, attend, s, j)
                    if heads:
                        score(at, 0, layer, heads[0], 0)
                        score(at, 1, layer, heads[0], 1)
                    if attend is not None:
                        if s > 0:
                            pv(at, attend, s - 1)
                        score_t(at, attend, s, 3)
                    if heads:
                        score(at, 2, layer, heads[0], 2)
                        score(at, 3, layer, heads[0], 3)
                    for n, h in enumerate(heads[1:]):
                        for qt in range(TT):
                            score(at, TT * (n + 1) + qt, layer, h, qt)
                    return
                if kind == "last":
                    pv(at, what, STEPS - 1)
                    return
                c = at["dense"]

                def bank(k):
                    wait(pe, dense_done, c.at(1, k - 1))
                    return DN[(c.index() + k) % 2]

                def by_token(k, rows, weights, tiles, depth):
                    psum = bank(k)
                    for n, t in enumerate(tiles):
                        for kt in range(depth):
                            ins = t_.matmul(psum[:, n * D:n * D + D], rows[:, kt, t * P:t * P + P],
                                            weights(kt), start=kt == 0, stop=kt == depth - 1)
                    ins.then_inc(dense_full, 1)

                if what in ("turn_a", "turn_m", "turn_1"):
                    wait(pe, norm_dve, at["norm"].at(4))
                    for ft in range(KT):
                        psum = bank(ft)
                        for t in range(TT):
                            ins = t_.transpose(psum[:, t * P:t * P + P], XN[:, t, ft * P:ft * P + P], ID32[:])
                        ins.then_inc(dense_full, 1)
                    marks["xt"] = c.at(1, 2)
                elif what in ("q0", "k0", "q1", "k1"):
                    side, n = "qk".index(what[0]), int(what[1])
                    wait(pe, dense_done, marks["xt"])
                    for t in range(2):
                        psum = bank(t)
                        for kt in range(KT):
                            lo = (2 * side + t) * P
                            ins = t_.matmul(psum[:], WQKV[n][:, kt, lo:lo + P], XT[:, kt, :],
                                            start=kt == 0, stop=kt == KT - 1)
                        ins.then_inc(dense_full, 1)
                elif what in ("v0", "v1"):
                    n = int(what[-1])
                    for tp in range(2):
                        by_token(tp, XT, lambda kt: WQKV[n][:, kt, 2 * D:3 * D], (2 * tp, 2 * tp + 1), KT)
                elif what in ("proj0", "proj1"):
                    n = int(what[-1])
                    wait(pe, scaled_dve, at["scale"].at())
                    for tp in range(2):
                        by_token(tp, OC, lambda kt: WP[n][:, kt, :], (2 * tp, 2 * tp + 1), KT)
                elif what in ("up_a", "up_b"):
                    wait(pe, dense_done, marks["xt"])
                    for k in range(4):
                        ht = k + 4 * (what == "up_b")
                        psum = bank(k)
                        for kt in range(KT):
                            ins = t_.matmul(psum[:], W1[:, kt, ht * P:ht * P + P], XT[:, kt, :],
                                            start=kt == 0, stop=kt == KT - 1)
                        ins.then_inc(dense_full, 1)
                    marks["hid"] = c.at(1, 4)
                elif what in ("down_a", "down_b"):
                    tp = "ab".index(what[-1])
                    wait(pe, dense_done, marks["hid"])
                    by_token(0, HID, lambda ht: W2[:, ht, :], (2 * tp, 2 * tp + 1), FT)
                elif what in ("max0", "max1"):
                    psum = bank(0).bitcast(BF16)
                    wait(pe, max_pool, at["maxima"].at(4, 4), apart=True)
                    for qt in range(TT):
                        ins = t_.transpose(psum[0:3 * H, qt * P:qt * P + P],
                                           NMP[:, qt, :, :].rearrange("p a h -> p (a h)"), ID16[:])
                    ins.then_inc(dense_full, 1)

            run_passes(pe, work, passed["pe"])


SILU_READY, ROWS_READY, FM_READY = 3, 20, 21
N_FIRST_LOAD, N_LOAD = 16, 8
N_CONSTS = 13

_SHAPE = (B, T, D)


def kernel(**inputs):
    import concourse.bacc as bacc
    from concourse.bass_utils import run_bass_kernel_spmd

    a = {k: np.asarray(v) for k, v in inputs.items()}

    def qk_order(w):
        return w.reshape(-1, H // 2, 2, HD).transpose(0, 2, 3, 1).reshape(-1, D)

    def out_order(w):
        return w.reshape(GROUPS, 2, 2, HD, D).transpose(1, 2, 3, 0, 4).reshape(D, D)

    w0 = a["L0_cond_Wqkv"]
    w1 = a["L1_cond_Wqkv"].reshape(H, HD, 3, D).transpose(2, 3, 0, 1).reshape(3, D, D)
    bq1 = a["L1_cond_bqkv"].reshape(H, HD, 3).transpose(2, 0, 1).reshape(3, D)
    arrays = {
        "x": a["x"],
        "cond_t": a["cond_1024"].T,
        "wqkv0": np.concatenate([qk_order(w0[:, 0:D]), qk_order(w0[:, D:2 * D]), w0[:, 2 * D:]], axis=1),
        "wproj0": out_order(a["L0_cond_Wproj"]),
        "w1": a["L0_cond_W1"],
        "w2": a["L0_cond_W2"],
        "wada": a["L0_cond_Wada"],
        "wqkv1": np.concatenate([qk_order(w1[0]), qk_order(w1[1]), w1[2]], axis=1),
        "wp1": out_order(a["L1_cond_Wp"].T),
        "wgb1": np.concatenate([a["L1_cond_Wg"].T, a["L1_cond_Wb"].T], axis=1),
        "b1": a["L0_cond_b1"],
        "b_qk1": np.concatenate([qk_order(bq1[0:1])[0], qk_order(bq1[1:2])[0]]),
        "bv1": bq1[2],
        "bp1": a["L1_cond_bp"],
    }
    for name in ("L0_cond_bada", "L0_cond_bproj", "L0_cond_b2", "L0_cond_g1", "L0_cond_be1",
                 "L0_cond_g2", "L0_cond_be2", "L1_cond_ln_g", "L1_cond_ln_b", "L1_cond_bg", "L1_cond_bb"):
        arrays[name] = a[name]
    arrays = {f"in_{k}": np.ascontiguousarray(v) for k, v in arrays.items()}
    nc = bacc.Bacc("TRN2", target_bir_lowering=False, num_devices=1, dynamic_dma_scratch_size=1024)
    args = {k: nc.dram_tensor(k, v.shape, mybir.dt.from_np(v.dtype), kind="ExternalInput").ap()
            for k, v in arrays.items()}
    names = list(args)
    out = nc.dram_tensor("out", _SHAPE, F32, kind="ExternalOutput").ap()
    two_layers(nc, *(args[k] for k in names[:14]), [args[k] for k in names[14:]], out)
    r = run_bass_kernel_spmd(nc, [arrays], core_ids=[0])
    return r.results[0]["out"]
```

```python
from contextlib import ExitStack

import concourse.bass as bass
import numpy as np
from concourse import mybir

F32 = mybir.dt.float32
BF16 = mybir.dt.bfloat16
ALU = mybir.AluOpType
ACT = mybir.ActivationFunctionType
AX = mybir.AxisListType

P = 128
B, T, D = 8, 512, 256
H = 16
HD = D // H
F = 4 * D
EPS = 1e-5
TT = T // P
KT = D // P
FT = F // P
GROUPS = H // 4
CUTS = 6
CUT_ROWS = CUTS * HD
ALL_ROWS = CUT_ROWS + 3
Q_PARTS = (0, 0, 0, 1, 1, 2)
K_PARTS = (0, 1, 2, 0, 1, 0)
VW = HD + 1
VROW = H * VW + 16
STEPS = GROUPS * TT
MASKED = -3.0e38
GATE_A, GATE_A_BIAS, GATE_M, GATE_M_BIAS, NORM1, SHIFT1, NORM_A, SHIFT_A, NORM_M, SHIFT_M = range(10)
BY_FEATURE = (NORM_A, SHIFT_A, NORM_M, SHIFT_M, NORM1, SHIFT1)

SLOT_X = """
    A recip0 A stackk0 A hold1 A A A scale0 proj0 norm_m A A A turn_m s s up_0 s up_1 s up_2 s up_3 s
    s up_4 s up_5 s up_6 s up_7 s a s p s down_0 s s down_1 s s s s down_2 s s s down_3 keep0 norm_1
    A A A s turn_1 s s s s a s p s s s s nm0 q1 stat_a norm_a A max0 k1 A last stackq1 stackk1 pack1
    v1"""
SLOT_Y = """
    A turn_a A A q0 recip1 a s p s s a s p s s scale1 a s p s s proj1 norm_o close1 k0 s s a s p s s a s p s
    a s p s a s p s s a s p s a s p s a s p s a s p s a s p s s nm1 A max1 last pack0 stackq0 v0"""
SLOT_X, SLOT_Y = (slot.replace("A", "a p").split() for slot in (SLOT_X, SLOT_Y))
BEHIND = {"recip0": 1, "hold1": 2, "scale0": 1, "proj0": 1, "norm_m": 1, "turn_m": 1, "keep0": 0,
          "norm_1": 1, "turn_1": 1, "q1": 1, "k1": 1, "v1": 1, "stackq1": 1, "stackk1": 1,
          "nm0": 0, "max0": 0, "pack1": 2, "recip1": 2, "scale1": 2, "proj1": 2, "norm_o": 2,
          "close1": 2, "stat_a": -1, "norm_a": -1, "turn_a": -1, "q0": -1, "k0": -1, "stackq0": -1,
          "stackk0": 0, "v0": -1, "pack0": 0, "nm1": 1, "max1": 1,
          **{f"up_{n}": 1 for n in range(FT)}, **{f"down_{n}": 1 for n in range(TT)}}
FIRST = ("stat_a", "norm_a", "turn_a", "q0", "k0", "stackq0", "v0")
ADDS = {"proj0": {"dense": 2, "res": 2}, "proj1": {"dense": 2}, "down_0": {}, "down_2": {},
        "down_1": {"dense": 1, "res": 1}, "down_3": {"dense": 1, "res": 1}, "nm0": {}, "nm1": {},
        "max0": {"dense": 1, "maxima": 1, "max0": 1}, "max1": {"dense": 1, "maxima": 1, "max1": 1},
        "hold1": {"hold": 1}, "recip0": {"sums": 1, "rows0": 1, "bias": 1},
        "recip1": {"sums": 1, "rows1": 1}, "pack0": {"pack": 1}, "pack1": {"pack": 1},
        "scale0": {"scale": 1}, "scale1": {"scale": 1},
        "keep0": {"keep": 1, "x_in": 1}, "close1": {"close": 1}, "stat_a": {},
        "stackq0": {}, "stackq1": {}, "stackk0": {"stack0": 1}, "stackk1": {"stack1": 1}}
for _n in ("turn_m", "turn_1", "turn_a", "v0", "v1"):
    ADDS[_n] = {"dense": 2}
for _n in ("q0", "k0", "q1", "k1"):
    ADDS[_n] = {"dense": 2, "high": 2, "low": 0 if _n[1] == "1" else 2, "low1": 2 if _n[1] == "1" else 0}
for _n in range(FT):
    ADDS[f"up_{_n}"] = {"dense": 1}
for _n in ("norm_m", "norm_1", "norm_a", "norm_o"):
    ADDS[_n] = {"norm": 1}
ADDS["norm_m"]["bias"] = 1
COUNTS = ("dense", "res", "bias", "maxima", "max0", "max1", "hold", "pack", "sums", "scale", "rows0",
          "rows1", "keep", "x_in", "close", "stack0", "stack1", "high", "low", "low1", "norm", "head", "step", "group",
          "scan")


class Loop:

    def __init__(self, eng, i, passed):
        self.eng, self.i, self.passed, self.registers = eng, i, passed, {}

    def apart(self):
        self.eng.sem_inc(self.passed, 1)

    def value(self, per, fixed):
        if per not in self.registers:
            pair = self.eng.alloc_register(f"grown_{per}"), self.eng.alloc_register(f"value_{per}")
            self.registers[per] = pair
            self.apart()
            self.eng.reg_mul(pair[0], self.i, per)
        grown, value = self.registers[per]
        if not fixed:
            return grown
        self.eng.reg_add(value, grown, fixed)
        return value


class Count:

    def __init__(self):
        self.n, self.start, self.loop, self.per = 0, 0, None, 0

    def enter(self, loop, first, per):
        self.start, self.n, self.loop, self.first, self.per = self.n, 0, loop, first, per

    def leave(self, passes):
        assert self.n == self.per, (self.n, self.per)
        self.n, self.loop = self.start + passes * self.per, None

    def at(self, times=1, add=0):
        if self.loop is None:
            return self.n * times + add
        fixed = (self.start - self.first * self.per + self.n) * times + add
        return self.loop, self.per * times, fixed

    def index(self):
        return self.n if self.loop is None else self.start + self.n


def per_pass():
    per = dict.fromkeys(COUNTS, 0)
    for chunk in SLOT_X + SLOT_Y:
        for name, n in ADDS.get(chunk, {}).items():
            per[name] += n
    for slot in (SLOT_X, SLOT_Y):
        assert slot.count("a") == slot.count("p") == STEPS and slot.count("s") == H * TT // 2, (slot.count("a"), slot.count("s"))
    per.update(head=2 * 4 * STEPS, step=2 * STEPS, group=2 * GROUPS, scan=2 * H * TT)
    return per


PER = per_pass()
FIRST_FULL, LAST_FULL = 3, B - 2


def wait(eng, sem, value, apart=False):
    if isinstance(value, int):
        if value > 0:
            eng.wait_ge(sem, value)
        return
    loop, per, fixed = value
    assert FIRST_FULL * per + fixed > 0, (per, fixed)
    eng.wait_ge(sem, loop.value(per, fixed))
    if apart:
        loop.apart()


def run_passes(eng, work, passed):
    at = {name: Count() for name in COUNTS}
    at["x_in"].n = 1
    for chunk in FIRST:
        do_chunk(at, work, chunk, 0)
    for i in range(FIRST_FULL):
        one_pass(at, work, i, i)
    with eng.Fori(FIRST_FULL, LAST_FULL + 1) as i:
        loop = Loop(eng, i, passed)
        for name in COUNTS:
            at[name].enter(loop, FIRST_FULL, PER[name])
        one_pass(at, work, i, None)
    for name in COUNTS:
        at[name].leave(LAST_FULL + 1 - FIRST_FULL)
    for i in range(LAST_FULL + 1, B + 2):
        one_pass(at, work, i, i)
    return at


def do_chunk(at, work, chunk, b):
    work(at, "chunk", chunk, b)
    for name, n in ADDS[chunk].items():
        at[name].n += n


def one_pass(at, work, i, number):

    def live(behind):
        return number is None or 0 <= number - behind < B

    for slot, attend, layer in ((SLOT_X, 1, 0), (SLOT_Y, 0, 1)):
        attending, scanning = live(2 if attend else 0), live(1 if layer else 0)
        step = half = 0
        for what in slot:
            if what == "a":
                if attending:
                    work(at, "attend", (step, attend, 0), i)
            elif what == "p":
                if attending:
                    work(at, "attend", (step, attend, 1), i)
                    at["head"].n += 4
                    at["step"].n += 1
                    at["group"].n += step > 0 and step % TT == 0
                    step += 1
            elif what == "s":
                if scanning:
                    work(at, "scan", (layer, half // 2, 2 * (half % 2)), i)
                    at["scan"].n += 2
                    half += 1
            elif what == "last":
                if attending:
                    work(at, "last", attend, i)
                    at["group"].n += 1
            elif live(BEHIND[what]):
                do_chunk(at, work, what, i - BEHIND[what])


def two_layers(nc, x, cond_t, wqkv0, wproj0, w1, w2, wada, wqkv1, wp1, wgb1, b1, b_qk1, bv1, bp1,
               vectors, out):
    ctx = ExitStack()
    with ctx:
        def sb(name, shape, dt=F32):
            return ctx.enter_context(nc.sbuf_tensor(name, shape, dt))

        def pb(name, shape, dt=F32):
            return ctx.enter_context(nc.psum_tensor(name, shape, dt))

        def sem(name):
            return ctx.enter_context(nc.semaphore(name))

        WQKV = [sb("WQKV0", [P, KT, 3 * D]), sb("WQKV1", [P, KT, 3 * D])]
        WP = [sb("WP0", [P, KT, D]), sb("WP1", [P, KT, D])]
        W1 = sb("W1", [P, KT, F])
        W2 = sb("W2", [P, FT, D])
        B1 = sb("B1", [P, FT])
        BQK1 = sb("BQK1", [P, 4])
        BV1 = sb("BV1", [P, D])
        BP1 = sb("BP1", [P, D])
        QS = [sb("QS0", [P, H, T], BF16), sb("QS1", [P, H, T], BF16)]
        KS = [sb("KS0", [P, H, T], BF16), sb("KS1", [P, H, T], BF16)]
        V = [sb("V0", [P, TT, VROW]), sb("V1", [P, TT, VROW])]
        E = sb("E", [P, 2, 4, T])
        HID = sb("HID", [P, FT, T])
        OE = sb("OE", [P, GROUPS, T])
        OC = sb("OC", [P, KT, T])
        RB = sb("RB", [P, KT, T])
        RS = sb("RS", [P, T // 8])
        RR = sb("RR", [P, T // 8])
        XIN = sb("XIN", [P, TT, D])
        XR = sb("XR", [P, TT, D])
        R1 = sb("R1", [P, TT, D])
        RH = sb("RH", [P, TT, D])
        TMP = sb("TMP", [P, TT, D])
        XN = sb("XN", [P, TT, D])
        OUT = sb("OUT", [P, TT, D])
        XT = sb("XT", [P, KT, T])
        X32 = sb("X32", [P, 2, T])
        PART = sb("PART", [P, 2, 3, 2, T], BF16)
        ROW0 = sb("ROW0", [P, 4, D])
        ROW1 = sb("ROW1", [P, 2, D])
        NT = sb("NT", [3 * H, T], BF16)
        MX = sb("MX", [P, TT, H])
        MR = sb("MR", [P, TT, H])
        NMP = sb("NMP", [P, TT, 3, H], BF16)
        STAT = sb("STAT", [P, TT, 6])
        MV = sb("MV", [P, TT, 2])
        VE = sb("VE", [P, TT])
        RSTD = sb("RSTD", [P, TT])
        HALF = sb("HALF", [P, TT])
        FM = sb("FM", [P, len(BY_FEATURE) * KT, B])
        ID32 = sb("ID32", [P, P])
        ID16 = sb("ID16", [P, P], BF16)
        CAUSAL = sb("CAUSAL", [P, P], BF16)
        CAUSAL_T = sb("CAUSAL_T", [P, P], BF16)
        CT = sb("CT", [P, KT, B])
        CE = sb("CE", [P, KT, B])
        CS = sb("CS", [P, KT, B])
        WADA = HID[:, 0:6, :].rearrange("p a b -> p (a b)").rearrange("p (k n) -> p k n", k=KT)
        WGB = E[:, 0, 0:2, :]
        MODS = OE[0:B, 0:3, :].rearrange("p a b -> p (a b)")
        GB = OE[0:B, 3, :]
        ROWS = QS[0].bitcast(F32)[0:B, 0:10, :]
        VEC = QS[1].bitcast(F32)[0:B, :, :].rearrange("p a b -> p (a b)")

        SC = [pb(f"SC{i}", [P, T]) for i in range(3)]
        DN = [pb(f"DN{i}", [P, T]) for i in range(2)]
        SX = [pb(f"SX{i}", [P, T]) for i in range(2)]
        OP = pb("OP", [P, T])

        sums_dram = nc.dram_tensor("recip_sums", (4, GROUPS, T), F32, kind="Internal").ap()
        rows_dram = nc.dram_tensor("row_vectors", (B, 6, D), F32, kind="Internal").ap()

        first_load = sem("first_load")
        other_load = sem("other_load")
        consts = sem("consts")
        set_act = sem("set_act")
        set_dve = sem("set_dve")
        set_pe = sem("set_pe")
        rows_out = sem("rows_out")
        x_dma = sem("x_dma")
        dense_full = sem("dense_full")
        dense_done = sem("dense_done")
        head_full = sem("head_full")
        exp_done = sem("exp_done")
        scan_full = sem("scan_full")
        scan_done = sem("scan_done")
        pv_done = sem("pv_done")
        out_act = sem("out_act")
        stat_dve = sem("stat_dve")
        rstd_pool = sem("rstd_pool")
        norm_dve = sem("norm_dve")
        high_act = sem("high_act")
        cut_dve = sem("cut_dve")
        cut_pool = sem("cut_pool")
        max_pool = sem("max_pool")
        max_dma = [sem("max_dma0"), sem("max_dma1")]
        stack_dma = [sem("stack_dma0"), sem("stack_dma1")]
        compact_dma = sem("compact_dma")
        recip_dve = sem("recip_dve")
        recip_dma = sem("recip_dma")
        spread_dma = sem("spread_dma")
        scaled_dve = sem("scaled_dve")
        row0_dma = sem("row0_dma")
        row1_dma = sem("row1_dma")
        bias_pool = sem("bias_pool")
        res_dve = sem("res_dve")
        hold_pool = sem("hold_pool")
        keep_dve = sem("keep_dve")
        close_pool = sem("close_pool")
        store_dma = sem("store_dma")

        passed = {name: sem(f"passed_{name}") for name in ("sp", "pool", "act", "dve", "pe")}

        block = ctx.enter_context(nc.Block())

        @block.sync
        def _(sp):
            sp.dma_start(CT[:], cond_t.rearrange("(k p) b -> p k b", p=P)).then_inc(first_load, 16)
            sp.dma_start(WADA, wada.rearrange("(k p) n -> p k n", p=P)).then_inc(first_load, 16)
            sp.dma_start(WGB, wgb1.rearrange("(k p) n -> p k n", p=P)).then_inc(first_load, 16)
            at_col = 0
            for v in vectors:
                n = v.shape[0]
                sp.dma_start(VEC[:, at_col:at_col + n],
                             v.unsqueeze(0).to_broadcast([B, n])).then_inc(first_load, 16)
                at_col += n
            sp.dma_start(WQKV[0][:], wqkv0.rearrange("(k p) n -> p k n", p=P)).then_inc(first_load, 16)
            sp.dma_start(WP[0][:], wproj0.rearrange("(k p) n -> p k n", p=P)).then_inc(first_load, 16)
            sp.dma_start(XIN[:], x[0].rearrange("(t p) d -> p t d", p=P)).then_inc(x_dma, 16)
            sp.dma_start(W1[:], w1.rearrange("(k p) n -> p k n", p=P)).then_inc(other_load, 16)
            sp.dma_start(W2[:], w2.rearrange("(k p) n -> p k n", p=P)).then_inc(other_load, 16)
            sp.dma_start(WQKV[1][:], wqkv1.rearrange("(k p) n -> p k n", p=P)).then_inc(other_load, 16)
            sp.dma_start(WP[1][:], wp1.rearrange("(k p) n -> p k n", p=P)).then_inc(other_load, 16)
            with nc.allow_non_contiguous_dma(reason="small bias vectors by feature"):
                sp.dma_start(B1[:], b1.rearrange("(k p) -> p k", p=P)).then_inc(other_load, 16)
                sp.dma_start(BQK1[:], b_qk1.rearrange("(k p) -> p k", p=P)).then_inc(other_load, 16)
            sp.dma_start(BV1[:], bv1.unsqueeze(0).to_broadcast([P, D])).then_inc(other_load, 16)
            sp.dma_start(BP1[:], bp1.unsqueeze(0).to_broadcast([P, D])).then_inc(other_load, 16)
            sp.wait_ge(set_dve, ROWS_READY)
            sp.dma_start(rows_dram, ROWS[:, 0:6, :]).then_inc(rows_out, 16)
            sp.wait_ge(rows_out, 16)

            def work(at, kind, what, b):
                if kind != "chunk":
                    return
                if what in ("pack0", "pack1"):
                    wait(sp, out_act, at["group"].at(), apart=True)
                    wait(sp, dense_full, at["dense"].at(), apart=True)
                    wait(sp, recip_dve, at["sums"].at(), apart=True)
                    sp.dma_start(RS[:], OE[HD:P:32, :, :]).then_inc(compact_dma, 16)
                    for j in range(4):
                        sp.dma_start(OC[64 * (j % 2):64 * (j % 2) + 64, j // 2, :],
                                     OE[32 * j:32 * j + HD, :, :]).then_inc(compact_dma, 16)
                elif what in ("recip0", "recip1"):
                    wait(sp, recip_dve, at["sums"].at(1, 1), apart=True)
                    wait(sp, spread_dma, at["sums"].at(64), apart=True)
                    sp.dma_start(sums_dram.rearrange("j g (c n) -> (j g c) n", c=8), RR[:])\
                        .then_inc(recip_dma, 16)
                    wait(sp, recip_dma, at["sums"].at(16, 16), apart=True)
                    wait(sp, scaled_dve, at["sums"].at(), apart=True)
                    for j in range(4):
                        sp.dma_start(RB[64 * (j % 2):64 * (j % 2) + 64, j // 2, :],
                                     sums_dram[j].unsqueeze(0).to_broadcast([HD, GROUPS, T]))\
                            .then_inc(spread_dma, 16)
                    if what == "recip0":
                        wait(sp, bias_pool, at["bias"].at(), apart=True)
                        wait(sp, res_dve, at["res"].at(), apart=True)
                        sp.dma_start(ROW0[:], rows_dram[bass.ds(b, 1), 0:4, :].to_broadcast([P, 4, D]))\
                            .then_inc(row0_dma, 16)
                    else:
                        wait(sp, close_pool, at["close"].at(3), apart=True)
                        sp.dma_start(ROW1[:], rows_dram[bass.ds(b, 1), 4:6, :].to_broadcast([P, 2, D]))\
                            .then_inc(row1_dma, 16)
                elif what == "keep0":
                    wait(sp, keep_dve, at["keep"].at(1, 1), apart=True)
                    if not isinstance(b, int) or b + 1 < B:
                        sp.dma_start(XIN[:], x[bass.ds(b + 1, 1)].rearrange("a (t p) d -> p (a t) d", p=P))\
                            .then_inc(x_dma, 16)
                elif what == "close1":
                    wait(sp, close_pool, at["close"].at(3, 3), apart=True)
                    sp.dma_start(out[bass.ds(b, 1)].rearrange("a (t p) d -> p (a t) d", p=P), OUT[:])\
                        .then_inc(store_dma, 16)
                elif what in ("stackq0", "stackq1", "stackk0", "stackk1"):
                    n, side = int(what[-1]), "qk".index(what[5])
                    wait(sp, high_act, at["high"].at(), apart=True)
                    if n == 0:
                        wait(sp, cut_pool, at["low"].at(), apart=True)
                    else:
                        wait(sp, cut_dve, at["low1"].at(), apart=True)
                    if side == 0:
                        wait(sp, pv_done, at["step"].at(), apart=True)
                    for r in range(CUTS):
                        sp.dma_start((QS, KS)[side][n][HD * r:HD * r + HD, :, :],
                                     PART[:, side, (Q_PARTS, K_PARTS)[side][r], :, :])\
                            .then_inc(stack_dma[n], 16)

            run_passes(sp, work, passed["sp"])
            sp.wait_ge(store_dma, 16 * B)

        @block.gpsimd
        def _(pool):
            g = nc.gpsimd
            g.memset(ID32[:], 0.0).then_inc(consts, 1)
            g.memset(ID16[:], 0.0).then_inc(consts, 1)
            g.memset(CAUSAL[:], 0.0).then_inc(consts, 1)
            g.memset(CAUSAL_T[:], 0.0).then_inc(consts, 1)
            pool.wait_ge(consts, 4)
            for m in (ID32, ID16):
                g.affine_select(out=m[:], in_=m[:], compare_op=ALU.not_equal, fill=1.0, base=0,
                                pattern=[[-1, P]], channel_multiplier=1).then_inc(consts, 1)
            g.affine_select(out=CAUSAL[:], in_=CAUSAL[:], compare_op=ALU.is_ge, fill=MASKED, base=0,
                            pattern=[[-1, P]], channel_multiplier=1).then_inc(consts, 1)
            g.affine_select(out=CAUSAL_T[:], in_=CAUSAL_T[:], compare_op=ALU.is_ge, fill=MASKED, base=0,
                            pattern=[[1, P]], channel_multiplier=-1).then_inc(consts, 1)
            g.memset(HALF[:], -0.5).then_inc(consts, 1)
            g.memset(V[0][:], 1.0).then_inc(consts, 1)
            g.memset(V[1][:], float(D) ** 0.5).then_inc(consts, 1)
            pool.wait_ge(consts, N_CONSTS - 2)
            g.memset(KS[0][CUT_ROWS:ALL_ROWS, :, :], 1.0).then_inc(consts, 1)
            pool.wait_ge(consts, N_CONSTS - 1)
            g.memset(KS[1][CUT_ROWS:ALL_ROWS, :, :], 1.0).then_inc(consts, 1)
            pool.wait_ge(consts, N_CONSTS)

            def work(at, kind, what, b):
                if kind != "chunk":
                    return
                if what in ("stat_a", "proj0", "down_3", "proj1"):
                    wait(pool, stat_dve, at["norm"].at(9, 9), apart=True)
                    g.tensor_tensor(RSTD[:], VE[:], HALF[:], ALU.pow).then_inc(rstd_pool, 1)
                elif what == "norm_m":
                    wait(pool, norm_dve, at["norm"].at(4, 4), apart=True)
                    g.tensor_tensor(XR[:], XR[:], ROW0[:, 3:4, :].to_broadcast([P, TT, D]), ALU.add)\
                        .then_inc(bias_pool, 1)
                elif what in ("q0", "k0"):
                    part = PART[:, "qk".index(what[0]), :, :, :]
                    c = at["low"]
                    wait(pool, dense_done, at["dense"].at(1, 2), apart=True)
                    g.tensor_scalar(part[:, 1], X32[:], 1.0, 0.0, ALU.mult, ALU.add).then_inc(cut_pool, 1)
                    wait(pool, cut_pool, c.at(1, 1), apart=True)
                    g.tensor_tensor(part[:, 2], X32[:], part[:, 1], ALU.subtract).then_inc(cut_pool, 1)
                elif what in ("nm0", "nm1"):
                    m = at["maxima"]
                    wait(pool, scan_done, at["scan"].at(), apart=True)
                    wait(pool, dense_full, at["dense"].at(), apart=True)
                    g.tensor_scalar(NMP[:, :, 0, :], MX[:], 1.0, 0.0, ALU.mult, ALU.add).then_inc(max_pool, 1)
                    wait(pool, max_pool, m.at(4, 1), apart=True)
                    g.tensor_tensor(MR[:], MX[:], NMP[:, :, 0, :], ALU.subtract).then_inc(max_pool, 1)
                    wait(pool, max_pool, m.at(4, 2), apart=True)
                    g.tensor_scalar(NMP[:, :, 1, :], MR[:], 1.0, 0.0, ALU.mult, ALU.add).then_inc(max_pool, 1)
                    wait(pool, max_pool, m.at(4, 3), apart=True)
                    g.tensor_tensor(NMP[:, :, 2, :], MR[:], NMP[:, :, 1, :], ALU.subtract).then_inc(max_pool, 1)
                elif what == "recip0":
                    wait(pool, row0_dma, at["rows0"].at(16, 16), apart=True)
                    wait(pool, keep_dve, at["keep"].at(), apart=True)
                    g.tensor_tensor(XR[:], XR[:], ROW0[:, 1:2, :].to_broadcast([P, TT, D]), ALU.add)\
                        .then_inc(bias_pool, 1)
                elif what == "hold1":
                    wait(pool, res_dve, at["res"].at(), apart=True)
                    wait(pool, other_load, 16 * N_LOAD, apart=True)
                    wait(pool, dense_done, at["dense"].at(), apart=True)
                    g.tensor_tensor(RH[:], R1[:], BP1[:].unsqueeze(1).to_broadcast([P, TT, D]), ALU.add)\
                        .then_inc(hold_pool, 1)
                elif what == "close1":
                    c = at["close"]
                    wait(pool, norm_dve, at["norm"].at(4), apart=True)
                    wait(pool, row1_dma, at["rows1"].at(16), apart=True)
                    g.tensor_tensor(OUT[:], OUT[:], ROW1[:, 0:1, :].to_broadcast([P, TT, D]), ALU.mult)\
                        .then_inc(close_pool, 1)
                    g.tensor_tensor(TMP[:], TMP[:], ROW1[:, 1:2, :].to_broadcast([P, TT, D]), ALU.add)\
                        .then_inc(close_pool, 1)
                    wait(pool, close_pool, c.at(3, 2), apart=True)
                    g.tensor_tensor(OUT[:], OUT[:], TMP[:], ALU.add).then_inc(close_pool, 1)

            run_passes(pool, work, passed["pool"])

        @block.scalar
        def _(act):
            a = nc.scalar
            act.wait_ge(first_load, 16 * N_FIRST_LOAD)
            a.activation(CE[:], CT[:], ACT.Exp, scale=-1.0).then_inc(set_act, 1)
            act.wait_ge(other_load, 16 * N_LOAD)
            act.wait_ge(set_dve, FM_READY)

            def take_out(at, g):
                wait(act, pv_done, at["step"].at())
                wait(act, compact_dma, at["pack"].at(80))
                a.activation(OE[:, g, :], OP[:], ACT.Copy).then_inc(out_act, 1)

            def work(at, kind, what, b):
                if kind == "attend":
                    s, attend, half = what
                    lo = P * (s % TT) if attend == 0 else 0
                    for j in ((0, 1, 2), (3,))[half]:
                        if j == 0:
                            wait(act, pv_done, at["step"].at(1, -1))
                        if j == 3 and s > 0 and s % TT == 0:
                            take_out(at, s // TT - 1)
                        wait(act, head_full, at["head"].at(1, j + 1))
                        a.activation(E[:, at["step"].index() % 2, j, lo:T], SC[(4 * s + j) % 3][:, lo:T],
                                     ACT.Exp, scale=HD ** -0.5 if attend == 0 else 1.0)\
                            .then_inc(exp_done, 1)
                    return
                if kind == "last":
                    take_out(at, GROUPS - 1)
                    return
                if kind != "chunk":
                    return
                c = at["dense"]

                def bank(k):
                    if k == 0:
                        wait(act, dense_done, c.at())
                    wait(act, dense_full, c.at(1, k + 1))
                    return DN[(c.index() + k) % 2]

                if what in ("turn_a", "turn_m", "turn_1"):
                    first = {"turn_a": 0, "turn_m": 2, "turn_1": 4}[what]
                    for ft in range(KT):
                        a.activation(XT[:, ft, :], bank(ft)[:], ACT.Identity,
                                     scale=FM[:, first * KT + ft, bass.ds(b, 1)],
                                     bias=FM[:, (first + 1) * KT + ft, bass.ds(b, 1)])\
                            .then_inc(dense_done, 1)
                elif what in ("q0", "k0", "q1", "k1"):
                    side = "qk".index(what[0])
                    wait(act, stack_dma[0], at["stack0"].at(192))
                    wait(act, stack_dma[1], at["stack1"].at(192))
                    for t in range(2):
                        part = PART[:, side, 0, t, :]
                        if what[1] == "0":
                            ins = a.activation(part, bank(t)[:], ACT.Copy)
                        else:
                            ins = a.activation(part, bank(t)[:], ACT.Identity,
                                               bias=BQK1[:, 2 * side + t:2 * side + t + 1])
                        ins.then_inc(high_act, 1)
                elif what.startswith("up_"):
                    ht = int(what[-1])
                    a.activation(HID[:, ht, :], bank(0)[:], ACT.Gelu, bias=B1[:, ht:ht + 1])\
                        .then_inc(dense_done, 1)
                elif what in ("max0", "max1"):
                    n = int(what[-1])
                    psum = bank(0)
                    wait(act, max_dma[0], at["max0"].at(16))
                    wait(act, max_dma[1], at["max1"].at(16))
                    a.activation(NT[:], psum.bitcast(BF16)[0:3 * H, 0:T], ACT.Copy).then_inc(dense_done, 1)
                    wait(act, dense_done, c.at(1, 1))
                    act.dma_start(QS[n][CUT_ROWS:ALL_ROWS, :, :], NT[:]).then_inc(max_dma[n], 16)

            run_passes(act, work, passed["act"])

        @block.vector
        def _(dve):
            v = nc.vector
            done = [0]

            def then(ins):
                done[0] += 1
                ins.then_inc(set_dve, 1)
                return done[0]

            dve.wait_ge(set_act, 1)
            n = then(v.tensor_scalar(CE[:], CE[:], 1.0, 1.0, ALU.mult, ALU.add))
            dve.wait_ge(set_dve, n)
            n = then(v.reciprocal(CE[:], CE[:]))
            dve.wait_ge(set_dve, n)
            n = then(v.tensor_tensor(CS[:], CT[:], CE[:], ALU.mult))
            assert n == SILU_READY
            dve.wait_ge(first_load, 16 * N_FIRST_LOAD)
            for c in range(3):
                dve.wait_ge(set_pe, c + 1)
                then(v.tensor_tensor(MODS[:, c * T:c * T + T], SC[c][0:B, :], VEC[:, c * T:c * T + T], ALU.add))
            dve.wait_ge(set_pe, 4)
            n = then(v.tensor_tensor(GB, OP[0:B, :], VEC[:, 6 * D + 8 * D:6 * D + 10 * D], ALU.add))
            dve.wait_ge(set_dve, n)

            def mod(k):
                return MODS[:, k * D:k * D + D]

            def vec(k):
                return VEC[:, (6 + k) * D:(7 + k) * D]

            (bproj, b2, g1, be1, g2, be2, ln_g, ln_b) = (vec(k) for k in range(8))
            (shift_a, scale_a, gate_a, shift_m, scale_m, gate_m) = (mod(k) for k in range(6))
            gamma, beta = GB[:, 0:D], GB[:, D:2 * D]
            then(v.tensor_copy(ROWS[:, GATE_A, :], gate_a))
            then(v.tensor_tensor(ROWS[:, GATE_A_BIAS, :], gate_a, bproj, ALU.mult))
            then(v.tensor_copy(ROWS[:, GATE_M, :], gate_m))
            then(v.tensor_tensor(ROWS[:, GATE_M_BIAS, :], gate_m, b2, ALU.mult))
            then(v.tensor_tensor(ROWS[:, NORM1, :], gamma, ln_g, ALU.mult))
            then(v.tensor_tensor(ROWS[:, SHIFT1, :], gamma, ln_b, ALU.mult))
            then(v.scalar_tensor_tensor(ROWS[:, NORM_A, :], scale_a, 1.0, g1, ALU.add, ALU.mult))
            then(v.scalar_tensor_tensor(ROWS[:, SHIFT_A, :], scale_a, 1.0, be1, ALU.add, ALU.mult))
            then(v.scalar_tensor_tensor(ROWS[:, NORM_M, :], scale_m, 1.0, g2, ALU.add, ALU.mult))
            n = then(v.scalar_tensor_tensor(ROWS[:, SHIFT_M, :], scale_m, 1.0, be2, ALU.add, ALU.mult))
            dve.wait_ge(set_dve, n)
            for row, plus in ((SHIFT1, beta), (SHIFT_A, shift_a), (SHIFT_M, shift_m)):
                n = then(v.tensor_tensor(ROWS[:, row, :], ROWS[:, row, :], plus, ALU.add))
            assert n == ROWS_READY
            dve.wait_ge(set_pe, 5)
            n = then(v.tensor_copy(FM[:], SX[0][:, 0:len(BY_FEATURE) * KT * B]
                                   .rearrange("p (k b) -> p k b", b=B)))
            assert n == FM_READY
            dve.wait_ge(set_dve, n)
            dve.wait_ge(consts, N_CONSTS)
            dve.wait_ge(other_load, 16 * N_LOAD)

            def scan(at, layer, h, qt):
                if h == 0 and qt == 0:
                    wait(dve, max_pool, at["maxima"].at(4))
                for k in range(2):
                    wait(dve, scan_full, at["scan"].at(1, k + 1))
                    w = (qt + k + 1) * P if layer == 0 else T
                    v.reduce_max(MX[:, qt + k, h:h + 1], SX[k][:, 0:w], AX.X, negate=True)\
                        .then_inc(scan_done, 1)

            def stats(at, src):
                c = at["norm"]
                for t in range(TT):
                    v.bn_stats(STAT[:, t, :], src[:, t, :]).then_inc(stat_dve, 1)
                wait(dve, stat_dve, c.at(9, 4), apart=True)
                for t in range(TT):
                    v.bn_aggr(MV[:, t, :], STAT[:, t, :]).then_inc(stat_dve, 1)
                wait(dve, stat_dve, c.at(9, 8), apart=True)
                v.tensor_scalar(VE[:], MV[:, :, 1], 1.0, EPS, ALU.mult, ALU.add).then_inc(stat_dve, 1)

            def work(at, kind, what, b):
                if kind == "scan":
                    scan(at, *what)
                    return
                if kind != "chunk":
                    return
                c = at["dense"]

                def bank(k):
                    if k == 0:
                        wait(dve, dense_done, c.at())
                    wait(dve, dense_full, c.at(1, k + 1))
                    return DN[(c.index() + k) % 2]

                if what == "stat_a":
                    wait(dve, x_dma, at["x_in"].at(16))
                    stats(at, XIN)
                elif what in ("norm_a", "norm_m", "norm_1", "norm_o"):
                    src = {"norm_a": XIN, "norm_m": XR, "norm_1": R1, "norm_o": TMP}[what]
                    dst = OUT if what == "norm_o" else XN
                    wait(dve, rstd_pool, at["norm"].at(1, 1))
                    if what == "norm_o":
                        wait(dve, store_dma, at["close"].at(16))
                    else:
                        wait(dve, dense_full, c.at())
                    for t in range(TT):
                        v.tensor_scalar(dst[:, t, :], src[:, t, :], MV[:, t, 0:1], RSTD[:, t:t + 1],
                                        ALU.subtract, ALU.mult).then_inc(norm_dve, 1)
                elif what in ("q0", "k0", "q1", "k1"):
                    side = "qk".index(what[0])
                    part = PART[:, side, :, :, :]
                    wait(dve, cut_pool, at["low"].at())
                    wait(dve, cut_dve, at["low1"].at())
                    wait(dve, dense_done, c.at())
                    for t in range(2):
                        wait(dve, high_act, at["high"].at(1, t + 1))
                        if what[1] == "0":
                            ins = v.tensor_tensor(X32[:, t, :], bank(t)[:], part[:, 0, t, :], ALU.subtract)
                        else:
                            ins = v.scalar_tensor_tensor(X32[:, t, :], bank(t)[:],
                                                         BQK1[:, 2 * side + t:2 * side + t + 1],
                                                         part[:, 0, t, :], ALU.add, ALU.subtract)
                        ins.then_inc(dense_done, 1)
                    if what[1] == "1":
                        lo = at["low1"]
                        wait(dve, dense_done, c.at(1, 2))
                        v.tensor_copy(part[:, 1], X32[:]).then_inc(cut_dve, 1)
                        wait(dve, cut_dve, lo.at(1, 1))
                        v.tensor_tensor(part[:, 2], X32[:], part[:, 1], ALU.subtract).then_inc(cut_dve, 1)
                elif what in ("v0", "v1"):
                    n = int(what[-1])
                    for tp in range(2):
                        psum = bank(tp)[:].rearrange("p (t h d) -> p t h d", t=2, d=HD)
                        for t in range(2):
                            dst = V[n][:, 2 * tp + t, 0:H * VW].rearrange("p (h e) -> p h e", e=VW)[:, :, 0:HD]
                            if n == 0:
                                ins = v.tensor_copy(dst, psum[:, t])
                            else:
                                ins = v.tensor_tensor(dst, psum[:, t],
                                                      BV1[:].rearrange("p (h d) -> p h d", d=HD), ALU.add)
                        ins.then_inc(dense_done, 1)
                elif what in ("proj0", "down_1", "down_3"):
                    wait(dve, row0_dma, at["rows0"].at(16))
                    wait(dve, bias_pool, at["bias"].at())
                    if what == "proj0":
                        wait(dve, close_pool, at["close"].at(3))
                    if what == "down_1":
                        wait(dve, hold_pool, at["hold"].at())
                    gate, dst = (0, XR) if what == "proj0" else (2, R1)
                    pairs = (0, 1) if what == "proj0" else (int(what[-1]) // 2,)
                    for n, tp in enumerate(pairs):
                        two = slice(2 * tp, 2 * tp + 2)
                        v.tensor_tensor(TMP[:, two, :], bank(n)[:].rearrange("p (t d) -> p t d", d=D),
                                        ROW0[:, gate:gate + 1, :].to_broadcast([P, 2, D]), ALU.mult)\
                            .then_inc(dense_done, 1)
                        wait(dve, dense_done, c.at(1, n + 1))
                        v.tensor_tensor(dst[:, two, :], XR[:, two, :], TMP[:, two, :], ALU.add)\
                            .then_inc(res_dve, 1)
                    if what != "down_1":
                        wait(dve, res_dve, at["res"].at(1, len(pairs)))
                        stats(at, dst)
                elif what == "proj1":
                    wait(dve, hold_pool, at["hold"].at())
                    for tp in range(2):
                        v.tensor_tensor(TMP[:, 2 * tp:2 * tp + 2, :], bank(tp)[:].rearrange("p (t d) -> p t d", d=D),
                                        RH[:, 2 * tp:2 * tp + 2, :], ALU.add).then_inc(dense_done, 1)
                    wait(dve, dense_done, c.at(1, 2))
                    stats(at, TMP)
                elif what in ("recip0", "recip1"):
                    wait(dve, compact_dma, at["pack"].at(80))
                    wait(dve, recip_dma, at["sums"].at(16))
                    v.reciprocal(RR[:], RS[:]).then_inc(recip_dve, 1)
                elif what in ("scale0", "scale1"):
                    wait(dve, spread_dma, at["sums"].at(64))
                    v.tensor_tensor(OC[:], OC[:], RB[:], ALU.mult).then_inc(scaled_dve, 1)
                elif what == "keep0":
                    wait(dve, x_dma, at["x_in"].at(16))
                    v.tensor_copy(XR[:], XIN[:]).then_inc(keep_dve, 1)

            run_passes(dve, work, passed["dve"])

        @block.tensor
        def _(pe):
            t_ = nc.tensor
            pe.wait_ge(first_load, 16 * N_FIRST_LOAD)
            pe.wait_ge(set_dve, SILU_READY)
            for c in range(3):
                for k in range(KT):
                    ins = t_.matmul(SC[c][0:B, :], CS[:, k, :], WADA[:, k, c * T:c * T + T],
                                    start=k == 0, stop=k == KT - 1)
                ins.then_inc(set_pe, 1)
            for k in range(KT):
                ins = t_.matmul(OP[0:B, :], CT[:, k, :], WGB[:, k, :], start=k == 0, stop=k == KT - 1)
            ins.then_inc(set_pe, 1)
            pe.wait_ge(consts, N_CONSTS)
            pe.wait_ge(set_dve, ROWS_READY)
            for n, row in enumerate(BY_FEATURE):
                for ft in range(KT):
                    c = (n * KT + ft) * B
                    ins = t_.transpose(SX[0][:, c:c + B], ROWS[:, row, ft * P:ft * P + P], ID32[0:B, 0:B])
            ins.then_inc(set_pe, 1)
            pe.wait_ge(set_dve, FM_READY)
            pe.wait_ge(other_load, 16 * N_LOAD)
            marks = {}

            def pv(at, attend, s):
                g, kt = s // TT, s % TT
                lo = P * kt if attend == 0 else 0
                wait(pe, exp_done, at["head"].at())
                if s == 0:
                    wait(pe, dense_done, at["dense"].at())
                if kt == 0:
                    wait(pe, out_act, at["group"].at())
                for j in range(4):
                    h = 4 * g + j
                    ins = t_.matmul(OP[32 * j:32 * j + 32, lo:T], V[attend][:, kt, h * VW:h * VW + 32],
                                    E[:, (at["step"].index() - 1) % 2, j, lo:T],
                                    start=kt == 0, stop=kt == TT - 1)
                ins.then_inc(pv_done, 1)

            def score_t(at, attend, s, j):
                g, kt = s // TT, s % TT
                h = 4 * g + j
                lo = P * kt if attend == 0 else 0
                u = 4 * s + j
                wait(pe, exp_done, at["head"].at(1, j if u == 0 else j - 2))
                ins = t_.matmul(SC[u % 3][:, lo:T], KS[attend][0:ALL_ROWS, h, kt * P:kt * P + P],
                                QS[attend][0:ALL_ROWS, h, lo:T], start=True, stop=attend == 1)
                if attend == 0:
                    ins = t_.matmul(SC[u % 3][:, lo:lo + P], ID16[:], CAUSAL_T[:], start=False, stop=True)
                ins.then_inc(head_full, 1)

            def scan(at, layer, h, qt):
                if h == 0 and qt == 0:
                    wait(pe, stack_dma[layer], at[f"stack{layer}"].at(192))
                for k in range(2):
                    q = qt + k
                    bank = SX[k]
                    wait(pe, scan_done, at["scan"].at(1, k - 1))
                    w = (q + 1) * P if layer == 0 else T
                    ins = t_.matmul(bank[:, 0:w], QS[layer][0:CUT_ROWS, h, q * P:q * P + P],
                                    KS[layer][0:CUT_ROWS, h, 0:w], start=True, stop=layer == 1)
                    if layer == 0:
                        ins = t_.matmul(bank[:, q * P:w], ID16[:], CAUSAL[:], start=False, stop=True)
                    ins.then_inc(scan_full, 1)

            def work(at, kind, what, b):
                if kind == "scan":
                    scan(at, *what)
                    return
                if kind == "attend":
                    s, attend, half = what
                    if half:
                        if s > 0:
                            pv(at, attend, s - 1)
                        score_t(at, attend, s, 3)
                        return
                    if s == 0:
                        wait(pe, max_dma[attend], at[f"max{attend}"].at(16))
                    for j in range(3):
                        score_t(at, attend, s, j)
                    return
                if kind == "last":
                    pv(at, what, STEPS - 1)
                    return
                c = at["dense"]

                def bank(k):
                    wait(pe, dense_done, c.at(1, k - 1))
                    return DN[(c.index() + k) % 2]

                def by_token(k, rows, weights, tiles, depth):
                    psum = bank(k)
                    for t in tiles:
                        for kt in range(depth):
                            ins = t_.matmul(psum[:, t % 2 * D:t % 2 * D + D], rows[:, kt, t * P:t * P + P],
                                            weights(kt), start=kt == 0, stop=kt == depth - 1)
                    if t % 2:
                        ins.then_inc(dense_full, 1)

                if what in ("turn_a", "turn_m", "turn_1"):
                    for ft in range(KT):
                        psum = bank(ft)
                        for t in range(TT):
                            if ft == 0:
                                wait(pe, norm_dve, at["norm"].at(4, t - 3))
                            ins = t_.transpose(psum[:, t * P:t * P + P], XN[:, t, ft * P:ft * P + P], ID32[:])
                        ins.then_inc(dense_full, 1)
                    marks["xt"] = c.at(1, 2)
                elif what in ("q0", "k0", "q1", "k1"):
                    side, n = "qk".index(what[0]), int(what[1])
                    wait(pe, dense_done, marks["xt"])
                    for t in range(2):
                        psum = bank(t)
                        for kt in range(KT):
                            lo = (2 * side + t) * P
                            ins = t_.matmul(psum[:], WQKV[n][:, kt, lo:lo + P], XT[:, kt, :],
                                            start=kt == 0, stop=kt == KT - 1)
                        ins.then_inc(dense_full, 1)
                elif what in ("v0", "v1"):
                    n = int(what[-1])
                    for tp in range(2):
                        by_token(tp, XT, lambda kt: WQKV[n][:, kt, 2 * D:3 * D], (2 * tp, 2 * tp + 1), KT)
                elif what in ("proj0", "proj1"):
                    n = int(what[-1])
                    wait(pe, scaled_dve, at["scale"].at())
                    for tp in range(2):
                        by_token(tp, OC, lambda kt: WP[n][:, kt, :], (2 * tp, 2 * tp + 1), KT)
                elif what.startswith("up_"):
                    ht = int(what[-1])
                    wait(pe, dense_done, marks["xt"])
                    psum = bank(0)
                    for kt in range(KT):
                        ins = t_.matmul(psum[:], W1[:, kt, ht * P:ht * P + P], XT[:, kt, :],
                                        start=kt == 0, stop=kt == KT - 1)
                    ins.then_inc(dense_full, 1)
                    marks["hid"] = c.at(1, 1)
                elif what.startswith("down_"):
                    wait(pe, dense_done, marks["hid"])
                    by_token(0, HID, lambda ht: W2[:, ht, :], (int(what[-1]),), FT)
                elif what in ("max0", "max1"):
                    psum = bank(0).bitcast(BF16)
                    wait(pe, max_pool, at["maxima"].at(4, 4), apart=True)
                    for qt in range(TT):
                        ins = t_.transpose(psum[0:3 * H, qt * P:qt * P + P],
                                           NMP[:, qt, :, :].rearrange("p a h -> p (a h)"), ID16[:])
                    ins.then_inc(dense_full, 1)

            run_passes(pe, work, passed["pe"])


SILU_READY, ROWS_READY, FM_READY = 3, 20, 21
N_FIRST_LOAD, N_LOAD = 16, 8
N_CONSTS = 13

_SHAPE = (B, T, D)


def kernel(**inputs):
    import concourse.bacc as bacc
    from concourse.bass_utils import run_bass_kernel_spmd

    a = {k: np.asarray(v) for k, v in inputs.items()}

    def qk_order(w):
        return w.reshape(-1, H // 2, 2, HD).transpose(0, 2, 3, 1).reshape(-1, D)

    def out_order(w):
        return w.reshape(GROUPS, 2, 2, HD, D).transpose(1, 2, 3, 0, 4).reshape(D, D)

    w0 = a["L0_cond_Wqkv"]
    w1 = a["L1_cond_Wqkv"].reshape(H, HD, 3, D).transpose(2, 3, 0, 1).reshape(3, D, D)
    bq1 = a["L1_cond_bqkv"].reshape(H, HD, 3).transpose(2, 0, 1).reshape(3, D)
    arrays = {
        "x": a["x"],
        "cond_t": a["cond_1024"].T,
        "wqkv0": np.concatenate([qk_order(w0[:, 0:D]), qk_order(w0[:, D:2 * D]), w0[:, 2 * D:]], axis=1),
        "wproj0": out_order(a["L0_cond_Wproj"]),
        "w1": a["L0_cond_W1"],
        "w2": a["L0_cond_W2"],
        "wada": a["L0_cond_Wada"],
        "wqkv1": np.concatenate([qk_order(w1[0]), qk_order(w1[1]), w1[2]], axis=1),
        "wp1": out_order(a["L1_cond_Wp"].T),
        "wgb1": np.concatenate([a["L1_cond_Wg"].T, a["L1_cond_Wb"].T], axis=1),
        "b1": a["L0_cond_b1"],
        "b_qk1": np.concatenate([qk_order(bq1[0:1])[0], qk_order(bq1[1:2])[0]]),
        "bv1": bq1[2],
        "bp1": a["L1_cond_bp"],
    }
    for name in ("L0_cond_bada", "L0_cond_bproj", "L0_cond_b2", "L0_cond_g1", "L0_cond_be1",
                 "L0_cond_g2", "L0_cond_be2", "L1_cond_ln_g", "L1_cond_ln_b", "L1_cond_bg", "L1_cond_bb"):
        arrays[name] = a[name]
    arrays = {f"in_{k}": np.ascontiguousarray(v) for k, v in arrays.items()}
    nc = bacc.Bacc("TRN2", target_bir_lowering=False, num_devices=1, dynamic_dma_scratch_size=1024)
    args = {k: nc.dram_tensor(k, v.shape, mybir.dt.from_np(v.dtype), kind="ExternalInput").ap()
            for k, v in arrays.items()}
    names = list(args)
    out = nc.dram_tensor("out", _SHAPE, F32, kind="ExternalOutput").ap()
    two_layers(nc, *(args[k] for k in names[:14]), [args[k] for k in names[14:]], out)
    r = run_bass_kernel_spmd(nc, [arrays], core_ids=[0])
    return r.results[0]["out"]
```
